# Optimizing a Trainium2 kernel written in Bass

```python
import numpy as np
import jax
import jax.numpy as jnp

def _softmax(x, axis=-1):
    return jax.nn.softmax(x, axis=axis)

def _gelu(x):
    return jax.nn.gelu(x, approximate=True)

def _silu(x):
    return jax.nn.silu(x)

def _sigmoid(x):
    return jax.nn.sigmoid(x)

def _layernorm(x, axis=-1, eps=1e-05):
    m = jnp.mean(x, axis=axis, keepdims=True)
    v = jnp.var(x, axis=axis, keepdims=True)
    return (x - m) / jnp.sqrt(v + eps)

def _scatter_add(tgt, idx, src, axis=0):
    return tgt.at[idx].add(src)

def _segment_sum(src, seg, n):
    return jax.ops.segment_sum(src, seg, n)
kernel_name = 'mk_vit_tower_cls_d2_tok_img512_r4_858d69'

def setup_inputs(seed: int=0):
    np.random.seed(seed)
    _w = jnp.asarray

    def _rec_inputs():
        import jax
        import jax.numpy as jnp
        _rk = jax.random.key(seed)
        x = -0.000153849 + 1.00027 * jax.random.normal(jax.random.fold_in(_rk, 1), (4, 3, 224, 224), jnp.float32)
        cls_tok = 0.02 * jax.random.normal(jax.random.fold_in(_rk, 5), (1, 1, 128), jnp.float32)
        return (x, cls_tok)
    x, cls_tok = _rec_inputs()

    def _L0_tok_setup():
        import jax, jax.numpy as jnp
        import numpy as np
        PATCH = 4
        EMBED = 128
        BATCH = 32
        key = jax.random.key(seed)
        k1, k2, k3 = jax.random.split(key, 3)
        x = jax.random.normal(k1, (BATCH, 3, 64, 64), dtype=jnp.float32)
        W = jax.random.normal(k2, (EMBED, PATCH * PATCH * 3), dtype=jnp.float32) * 0.02
        b = jnp.zeros((EMBED,), dtype=jnp.float32)
        cls = jax.random.normal(k3, (1, 1, EMBED), dtype=jnp.float32)
        return {'x': x, 'W': W, 'b': b, 'cls': cls}
    _L0_tok_all = _L0_tok_setup()
    _L0_tok_in = {k: v for k, v in _L0_tok_all.items() if k in ('W', 'b', 'cls')}
    del _L0_tok_all

    def _L0_attn_setup():
        import jax, jax.numpy as jnp
        import numpy as np
        B, T, D_MODEL = (2, 256, 128)
        EXPAND = 2
        D_INNER = D_MODEL * EXPAND
        STATE = 16
        K_CONV = 4

        def _silu(v):
            return v * jax.nn.sigmoid(v)
        key = jax.random.key(seed)
        ks = jax.random.split(key, 10)
        sc = lambda k, shape: jax.random.normal(k, shape, jnp.float32) * 0.02
        return {'x': jax.random.normal(ks[0], (B, T, D_MODEL), jnp.float32), 'ln_g': jnp.ones((D_MODEL,), jnp.float32), 'ln_b': jnp.zeros((D_MODEL,), jnp.float32), 'W_in': sc(ks[1], (2 * D_INNER, D_MODEL)), 'conv_w': sc(ks[2], (D_INNER, 1, K_CONV)), 'conv_b': jnp.zeros((D_INNER,), jnp.float32), 'W_B': sc(ks[3], (STATE, D_INNER)), 'W_C': sc(ks[4], (STATE, D_INNER)), 'W_dt': sc(ks[5], (D_INNER, D_INNER)), 'b_dt': jax.random.uniform(ks[6], (D_INNER,), jnp.float32, -4.0, -1.0), 'log_A': jnp.broadcast_to(jnp.log(jnp.arange(1, STATE + 1, dtype=jnp.float32)), (D_INNER, STATE)), 'W_out': sc(ks[7], (D_MODEL, D_INNER))}
    _L0_attn_all = _L0_attn_setup()
    _L0_attn_in = {k: v for k, v in _L0_attn_all.items() if k in ('ln_g', 'ln_b', 'W_in', 'conv_w', 'conv_b', 'W_B', 'W_C', 'W_dt', 'b_dt', 'log_A', 'W_out')}
    del _L0_attn_all

    def _L0_ffn_setup():
        import jax, jax.numpy as jnp
        import numpy as np
        B, T, D = (4, 2048, 128)
        E, F, CAP = (8, 512, 1024)
        key = jax.random.key(seed)
        ks = jax.random.split(key, 6)
        s = 0.02
        return {'x': jax.random.normal(ks[0], (B, T, D), dtype=jnp.float32), 'Wr': jax.random.normal(ks[1], (D, E), dtype=jnp.float32) * s, 'W1': jax.random.normal(ks[2], (E, D, F), dtype=jnp.float32) * s, 'b1': jax.random.normal(ks[3], (E, F), dtype=jnp.float32) * s, 'W2': jax.random.normal(ks[4], (E, F, D), dtype=jnp.float32) * s, 'b2': jax.random.normal(ks[5], (E, D), dtype=jnp.float32) * s}
    _L0_ffn_all = _L0_ffn_setup()
    _L0_ffn_in = {k: v for k, v in _L0_ffn_all.items() if k in ('Wr', 'W1', 'b1', 'W2', 'b2')}
    del _L0_ffn_all

    def _L1_attn_setup():
        import jax, jax.numpy as jnp
        import numpy as np
        H = 8
        W = 64
        SHIFT = True
        DIM = 128
        SCALE = (DIM // H) ** (-0.5)
        key = jax.random.key(seed)
        k1, k2, k3, k4 = jax.random.split(key, 4)
        x = jax.random.normal(k1, (8, 1024, DIM), dtype=jnp.float32)
        w_qkv = jax.random.normal(k2, (3 * DIM, DIM), dtype=jnp.float32) * 0.02
        w_proj = jax.random.normal(k3, (DIM, DIM), dtype=jnp.float32) * 0.02
        b_proj = jax.random.normal(k4, (DIM,), dtype=jnp.float32) * 0.02
        return {'x': x, 'w_qkv': w_qkv, 'w_proj': w_proj, 'b_proj': b_proj}
    _L1_attn_all = _L1_attn_setup()
    _L1_attn_in = {k: v for k, v in _L1_attn_all.items() if k in ('w_qkv', 'w_proj', 'b_proj')}
    del _L1_attn_all

    def _L1_ffn_setup():
        import jax, jax.numpy as jnp
        import numpy as np
        B, T, C = (8, 256, 128)
        H = 256
        G, EG = (2, 4)
        E = G * EG
        K = 2
        LN_EPS = 1e-05

        def _swiglu(x):
            a, b = jnp.split(x, 2, axis=-1)
            return jax.nn.silu(a) * b
        key = jax.random.key(seed)
        ks = jax.random.split(key, 8)
        n = lambda k, shape, s: jax.random.normal(k, shape, dtype=jnp.float32) * s
        return {'x': n(ks[0], (B, T, C), 1.0), 'ln_scale': jnp.ones((C,), jnp.float32), 'ln_bias': jnp.zeros((C,), jnp.float32), 'shared_in_w': n(ks[1], (2 * H, C), 0.02), 'shared_out_w': n(ks[2], (C, H), 0.02), 'shared_out_b': jnp.zeros((C,), jnp.float32), 'expert_in_w': n(ks[3], (2 * H, C), 0.02), 'expert_out_weight': n(ks[4], (E, C, H), 0.02), 'expert_out_bias': jnp.zeros((E, C), jnp.float32), 'group_gate_w': n(ks[5], (G, C), 0.02), 'expert_gate_w': n(ks[6], (E, C), 0.02), 'group_bias': jnp.zeros((G,), jnp.float32), 'expert_bias': jnp.zeros((E,), jnp.float32)}
    _L1_ffn_all = _L1_ffn_setup()
    _L1_ffn_in = {k: v for k, v in _L1_ffn_all.items() if k in ('ln_scale', 'ln_bias', 'shared_in_w', 'shared_out_w', 'shared_out_b', 'expert_in_w', 'expert_out_weight', 'expert_out_bias', 'group_gate_w', 'expert_gate_w', 'group_bias', 'expert_bias')}
    del _L1_ffn_all
    return {'x': x, 'cls_tok': cls_tok, 'L0_tok_W': _L0_tok_in['W'], 'L0_tok_b': _L0_tok_in['b'], 'L0_tok_cls': _L0_tok_in['cls'], 'L0_attn_ln_g': _L0_attn_in['ln_g'], 'L0_attn_ln_b': _L0_attn_in['ln_b'], 'L0_attn_W_in': _L0_attn_in['W_in'], 'L0_attn_conv_w': _L0_attn_in['conv_w'], 'L0_attn_conv_b': _L0_attn_in['conv_b'], 'L0_attn_W_B': _L0_attn_in['W_B'], 'L0_attn_W_C': _L0_attn_in['W_C'], 'L0_attn_W_dt': _L0_attn_in['W_dt'], 'L0_attn_b_dt': _L0_attn_in['b_dt'], 'L0_attn_log_A': _L0_attn_in['log_A'], 'L0_attn_W_out': _L0_attn_in['W_out'], 'L0_ffn_Wr': _L0_ffn_in['Wr'], 'L0_ffn_W1': _L0_ffn_in['W1'], 'L0_ffn_b1': _L0_ffn_in['b1'], 'L0_ffn_W2': _L0_ffn_in['W2'], 'L0_ffn_b2': _L0_ffn_in['b2'], 'L1_attn_w_qkv': _L1_attn_in['w_qkv'], 'L1_attn_w_proj': _L1_attn_in['w_proj'], 'L1_attn_b_proj': _L1_attn_in['b_proj'], 'L1_ffn_ln_scale': _L1_ffn_in['ln_scale'], 'L1_ffn_ln_bias': _L1_ffn_in['ln_bias'], 'L1_ffn_shared_in_w': _L1_ffn_in['shared_in_w'], 'L1_ffn_shared_out_w': _L1_ffn_in['shared_out_w'], 'L1_ffn_shared_out_b': _L1_ffn_in['shared_out_b'], 'L1_ffn_expert_in_w': _L1_ffn_in['expert_in_w'], 'L1_ffn_expert_out_weight': _L1_ffn_in['expert_out_weight'], 'L1_ffn_expert_out_bias': _L1_ffn_in['expert_out_bias'], 'L1_ffn_group_gate_w': _L1_ffn_in['group_gate_w'], 'L1_ffn_expert_gate_w': _L1_ffn_in['expert_gate_w'], 'L1_ffn_group_bias': _L1_ffn_in['group_bias'], 'L1_ffn_expert_bias': _L1_ffn_in['expert_bias']}

def reference(x, cls_tok, L0_tok_W, L0_tok_b, L0_tok_cls, L0_attn_ln_g, L0_attn_ln_b, L0_attn_W_in, L0_attn_conv_w, L0_attn_conv_b, L0_attn_W_B, L0_attn_W_C, L0_attn_W_dt, L0_attn_b_dt, L0_attn_log_A, L0_attn_W_out, L0_ffn_Wr, L0_ffn_W1, L0_ffn_b1, L0_ffn_W2, L0_ffn_b2, L1_attn_w_qkv, L1_attn_w_proj, L1_attn_b_proj, L1_ffn_ln_scale, L1_ffn_ln_bias, L1_ffn_shared_in_w, L1_ffn_shared_out_w, L1_ffn_shared_out_b, L1_ffn_expert_in_w, L1_ffn_expert_out_weight, L1_ffn_expert_out_bias, L1_ffn_group_gate_w, L1_ffn_expert_gate_w, L1_ffn_group_bias, L1_ffn_expert_bias):
    import jax
    import jax.numpy as jnp

    def _L0_tok_ref(x, W, b, cls):
        import jax, jax.numpy as jnp
        import numpy as np
        PATCH = 4
        EMBED = 128
        BATCH = 32
        B, C, H, Wd = x.shape
        p = PATCH
        nh, nw = (H // p, Wd // p)
        patches = x.reshape(B, C, nh, p, nw, p)
        patches = patches.transpose(0, 2, 4, 1, 3, 5)
        patches = patches.reshape(B, nh * nw, C * p * p)
        proj = jnp.einsum('bld,ed->ble', patches, W) + b
        cls_tok = jnp.broadcast_to(cls, (B, 1, EMBED))
        return jnp.concatenate([cls_tok, proj], axis=1)

    def _L0_attn_ref(x, ln_g, ln_b, W_in, conv_w, conv_b, W_B, W_C, W_dt, b_dt, log_A, W_out):
        import jax, jax.numpy as jnp
        import numpy as np
        B, T, D_MODEL = (2, 256, 128)
        EXPAND = 2
        D_INNER = D_MODEL * EXPAND
        STATE = 16
        K_CONV = 4

        def _silu(v):
            return v * jax.nn.sigmoid(v)
        residual = x
        mu = x.mean(-1, keepdims=True)
        var = x.var(-1, keepdims=True)
        xn = (x - mu) * jax.lax.rsqrt(var + 1e-05) * ln_g + ln_b
        xz = xn @ W_in.T
        x_main, z = jnp.split(xz, 2, axis=-1)
        xc = jnp.transpose(x_main, (0, 2, 1))
        xc = jax.lax.conv_general_dilated(xc, conv_w, window_strides=(1,), padding=[(K_CONV - 1, 0)], dimension_numbers=('NCH', 'OIH', 'NCH'), feature_group_count=D_INNER) + conv_b[None, :, None]
        x_main = _silu(jnp.transpose(xc, (0, 2, 1)))
        xf = x_main.astype(jnp.float32)
        Bt = xf @ W_B.T
        Ct = xf @ W_C.T
        dt = jax.nn.softplus(xf @ W_dt.T + b_dt)
        A = -jnp.exp(log_A)
        dA = jnp.exp(A[None, None] * dt[..., None])
        dBx = dt[..., None] * Bt[:, :, None, :] * xf[..., None]

        def comb(c1, c2):
            a1, b1 = c1
            a2, b2 = c2
            return (a1 * a2, a2 * b1 + b2)
        _, h = jax.lax.associative_scan(comb, (dA, dBx), axis=1)
        y = (h * Ct[:, :, None, :]).sum(-1).astype(x.dtype)
        out = y * _silu(z) @ W_out.T
        return residual + out

    def _L0_ffn_ref(x, Wr, W1, b1, W2, b2):
        import jax, jax.numpy as jnp
        import numpy as np
        B, T, D = (4, 2048, 128)
        E, F, CAP = (8, 512, 1024)
        Bb, Tt, Dd = x.shape
        N = Bb * Tt
        C = min(CAP, N)
        x_flat = x.reshape(N, Dd)
        logits = x_flat @ Wr
        probs = jax.nn.softmax(logits, axis=0)
        vals, idx = jax.lax.top_k(probs.T, C)
        selected = x_flat[idx]
        h = jax.nn.gelu(jnp.einsum('ecd,edf->ecf', selected, W1) + b1[:, None, :], approximate=False)
        out_e = jnp.einsum('ecf,efd->ecd', h, W2) + b2[:, None, :]
        weighted = vals[..., None] * out_e
        output = jnp.zeros_like(x_flat).at[idx.reshape(-1)].add(weighted.reshape(-1, Dd))
        return output.reshape(Bb, Tt, Dd)

    def _L1_attn_ref(x, w_qkv, w_proj, b_proj):
        import jax, jax.numpy as jnp
        import numpy as np
        H = 8
        W = 64
        SHIFT = True
        DIM = 128
        SCALE = (DIM // H) ** (-0.5)
        B, N, C = x.shape
        if SHIFT:
            x = jnp.roll(x, -W // 2, axis=1)
        pad = (W - N % W) % W
        if pad:
            x = jnp.pad(x, ((0, 0), (0, pad), (0, 0)))
        nw = x.shape[1] // W
        xw = x.reshape(B * nw, W, C)
        qkv = xw @ w_qkv.T
        qkv = qkv.reshape(B * nw, W, 3, H, C // H)
        q, k, v = (qkv[:, :, 0], qkv[:, :, 1], qkv[:, :, 2])
        attn = jnp.einsum('bwhd,bwgd->bwhg', q, k) * SCALE
        attn = jax.nn.softmax(attn, axis=-1)
        out = jnp.einsum('bwhg,bwgd->bwhd', attn, v)
        out = out.transpose(0, 2, 1, 3).reshape(B * nw, W, C)
        out = out @ w_proj.T + b_proj
        out = out.reshape(B, nw * W, C)[:, :N]
        if SHIFT:
            out = jnp.roll(out, W // 2, axis=1)
        return out

    def _L1_ffn_ref(x, ln_scale, ln_bias, shared_in_w, shared_out_w, shared_out_b, expert_in_w, expert_out_weight, expert_out_bias, group_gate_w, expert_gate_w, group_bias, expert_bias):
        import jax, jax.numpy as jnp
        import numpy as np
        B, T, C = (8, 256, 128)
        H = 256
        G, EG = (2, 4)
        E = G * EG
        K = 2
        LN_EPS = 1e-05

        def _swiglu(x):
            a, b = jnp.split(x, 2, axis=-1)
            return jax.nn.silu(a) * b
        Bx, Tx, Cx = x.shape
        S = Bx * Tx
        flat = x.reshape(S, Cx)
        mu = flat.mean(-1, keepdims=True)
        var = ((flat - mu) ** 2).mean(-1, keepdims=True)
        flat = (flat - mu) * jax.lax.rsqrt(var + LN_EPS) * ln_scale + ln_bias
        h_shared = _swiglu(flat @ shared_in_w.T)
        out_shared = h_shared @ shared_out_w.T + shared_out_b
        g_logits = flat @ group_gate_w.T + group_bias
        g_idx = jnp.argmax(g_logits, axis=-1)
        e_logits = (flat @ expert_gate_w.T).reshape(S, G, EG)
        e_sel = jnp.take_along_axis(e_logits, g_idx[:, None, None], axis=1)[:, 0, :]
        e_sel = e_sel + expert_bias.reshape(G, EG)[g_idx]
        e_probs = jax.nn.softmax(e_sel, axis=-1)
        topv, topi = jax.lax.top_k(e_probs, K)
        topv = topv / (topv.sum(-1, keepdims=True) + 1e-08)
        disp = g_idx[:, None] * EG + topi
        h_expert = _swiglu(flat @ expert_in_w.T)
        rows = jnp.arange(S)[:, None]
        comb = jnp.zeros((S, E), flat.dtype).at[rows, disp].add(topv)
        cnt = jnp.zeros((S, E), flat.dtype).at[rows, disp].add(1.0)
        routed = cnt @ expert_out_bias
        for e in range(E):
            routed = routed + comb[:, e:e + 1] * (h_expert @ expert_out_weight[e].T)
        return (out_shared + routed).reshape(Bx, Tx, Cx)
    h = _L0_tok_ref(x, L0_tok_W, L0_tok_b, L0_tok_cls)
    h = jnp.concatenate([jnp.broadcast_to(cls_tok, (h.shape[0], 1, h.shape[2])), h], axis=1)
    h = h + _L0_attn_ref(_layernorm(h, axis=-1), L0_attn_ln_g, L0_attn_ln_b, L0_attn_W_in, L0_attn_conv_w, L0_attn_conv_b, L0_attn_W_B, L0_attn_W_C, L0_attn_W_dt, L0_attn_b_dt, L0_attn_log_A, L0_attn_W_out)
    h = h + _L0_ffn_ref(_layernorm(h, axis=-1), L0_ffn_Wr, L0_ffn_W1, L0_ffn_b1, L0_ffn_W2, L0_ffn_b2)
    h = h + _L1_attn_ref(_layernorm(h, axis=-1), L1_attn_w_qkv, L1_attn_w_proj, L1_attn_b_proj)
    h = h + _L1_ffn_ref(_layernorm(h, axis=-1), L1_ffn_ln_scale, L1_ffn_ln_bias, L1_ffn_shared_in_w, L1_ffn_shared_out_w, L1_ffn_shared_out_b, L1_ffn_expert_in_w, L1_ffn_expert_out_weight, L1_ffn_expert_out_bias, L1_ffn_group_gate_w, L1_ffn_expert_gate_w, L1_ffn_group_bias, L1_ffn_expert_bias)
    return h

_drawn_inputs = setup_inputs


def setup_inputs(seed=0):
    import zlib

    import numpy as np

    out = dict(_drawn_inputs(seed))
    spreads = {'L0_tok_b': (0.0, 0.1),
     'L0_attn_ln_g': (1.0, 0.6),
     'L0_attn_ln_b': (0.0, 0.8),
     'L0_attn_conv_b': (0.0, 0.8),
     'L1_ffn_ln_scale': (1.0, 0.2),
     'L1_ffn_ln_bias': (0.0, 0.1),
     'L1_ffn_shared_out_b': (0.0, 0.8),
     'L1_ffn_expert_out_bias': (0.0, 0.628),
     'L1_ffn_group_bias': (0.0, 0.1),
     'L1_ffn_expert_bias': (0.0, 0.1)}
    factors = {'cls_tok': 48.238,
     'L0_attn_W_in': 8.0,
     'L0_attn_conv_w': 8.0,
     'L0_attn_W_B': 8.0,
     'L0_attn_W_C': 8.0,
     'L0_attn_W_dt': 8.0,
     'L0_attn_b_dt': 8.0,
     'L0_attn_log_A': 8.0,
     'L0_attn_W_out': 8.0,
     'L0_ffn_Wr': 64.0,
     'L0_ffn_W1': 64.0,
     'L0_ffn_b1': 64.0,
     'L0_ffn_W2': 64.0,
     'L0_ffn_b2': 200.0,
     'L1_ffn_shared_in_w': 7.672,
     'L1_ffn_shared_out_w': 7.713,
     'L1_ffn_expert_in_w': 8.0,
     'L1_ffn_expert_out_weight': 8.0,
     'L0_tok_cls': 17.52}
    for name, (base, spread) in spreads.items():
        noise = np.random.default_rng([zlib.crc32(name.encode()), seed]).standard_normal(out[name].shape)
        drawn = base * np.exp(spread * noise) if base else spread * noise
        out[name] = jnp.asarray(drawn.astype(out[name].dtype))
    for name, factor in factors.items():
        out[name] = (out[name] * factor).astype(out[name].dtype)
    return out
```

```python
from contextlib import ExitStack

import numpy as np

import concourse.bass as bass
from concourse import mybir
from concourse.alu_op_type import AluOpType as ALU

F32 = mybir.dt.float32
BF16 = mybir.dt.bfloat16
I32 = mybir.dt.int32
U32 = mybir.dt.uint32
ACT = mybir.ActivationFunctionType
AX = mybir.AxisListType
ds = bass.ds

P = 128
BATCH = 4
D = 128
DI = 256
NS = 16
KC = 4
PV = 48
NPATCH = 3136
T = NPATCH + 2
NTOK = BATCH * T
W = 448
NCH = NPATCH // W
TT = 112
NT = W // TT
SHIFT = 32
RPI = 3200
RB = RPI
ROWS = BATCH * RB + SHIFT
EPS = 1e-5
E0 = 8
CAP = 1024
FF = 512
SPAN = 785
NLG = 16 * SPAN
STEPS = 2 * NS
H_RING, DA_RING, DBX_RING, HC_RING, CS_RING = 16, 4, 3, 8, 4
SUM_LAG = 6

PRE_USES = (("tok", "xm1", "z0", "dt0"), ("mean", "var", "xm0", "z1", "bc", "dt1"))
POST_USES = (("out", "mean2", "logit", "trh"), ("var2", "trn"))
ORDER = ("tok", "mean", "out", "var", "mean2", "xm0", "xm1", "var2", "z0", "z1", "logit", "bc", "dt0", "dt1",
         "trh", "trn")


def need(eng, sem, value):
    if isinstance(value, int) and value <= 0:
        return
    eng.wait_ge(sem, value)


class Turn:

    def __init__(self, q, slot, w=W, scan=True, pre=True, post=True, post_w=W, pre_w=W, pre_at=None, post_at=None,
                 fresh=False, reset=False):
        self.first = isinstance(q, int) and q == 0
        self.q, self.slot, self.w, self.scan, self.pre, self.post = q, slot, w, scan, pre, post
        self.pre_w, self.post_w = pre_w, post_w
        self.pre_at, self.post_at = pre_at, post_at
        self.fresh = fresh
        self.reset = reset

    def bank_of(self, use):
        return 0 if use in PRE_USES[0] + POST_USES[0] else 1

    def nth(self, use):
        b = self.bank_of(use)
        mine = [u for u in ORDER if u in (PRE_USES[b] if self.pre else ()) + (POST_USES[b] if self.post else ())
                and not (u == "tok" and self.pre_w != W)]
        before = (len(PRE_USES[b]) - (b == 0)) * (self.has(0)) + len(PRE_USES[b]) * (self.has(1))
        if self.has(2):
            before = before + (self.q - 1) * (len(PRE_USES[b]) + len(POST_USES[b]))
        if isinstance(self.q, int) and self.q == 29:
            before -= len(PRE_USES[b])
        return before + mine.index(use)

    def has(self, n):
        return (not isinstance(self.q, int)) or self.q + 1 > n


def phase_a_turns(engine):
    yield Turn(-1, 0, scan=False, post=False, pre_w=2)
    yield Turn(0, 1, w=2, post=False, pre_at=(0, 0), fresh=True)
    for pair in range(BATCH // 2):
        q0 = 2 * NCH * pair
        last = pair == BATCH // 2 - 1
        yield Turn(q0 + 1, 0, pre_at=(2 * pair + 1, 0), post_w=2 if pair == 0 else W,
                   post_at=(2 * pair - 1, NCH - 1))
        with engine.Fori(0, NCH - 1) as c:
            yield Turn(q0 + 2 + c * 2, 1, pre_at=(2 * pair, c + 1), post_at=(2 * pair, c))
            yield Turn(q0 + 3 + c * 2, 0, pre_at=(2 * pair + 1, c + 1), post_at=(2 * pair + 1, c))
        yield Turn(q0 + 2 * NCH, 1, pre=not last, pre_at=(2 * pair + 2, 0), post_at=(2 * pair, NCH - 1),
                   fresh=not last, reset=not last)
    yield Turn(2 * NCH * (BATCH // 2) + 1, 0, scan=False, pre=False, post_at=(BATCH - 1, NCH - 1))


def build(nc, a, out, upto="C", debug=None):
    debug = debug or {}
    with ExitStack() as ctx:
        def sb(name, shape, dt=F32):
            return ctx.enter_context(nc.sbuf_tensor(name, shape, dt))

        def ps(name, shape, dt=F32):
            return ctx.enter_context(nc.psum_tensor(name, shape, dt))

        def sem(name):
            return ctx.enter_context(nc.semaphore(name))

        def dram(name, shape, dt=F32):
            return debug[name] if name in debug else nc.dram_tensor(name, shape, dt, kind="Internal").ap()

        h_rows = dram("h_rows", [ROWS, D])
        n_rows = dram("n_rows", [ROWS, D])
        logits = dram("logits", [E0, NLG])
        block = ctx.enter_context(nc.Block())
        progs = {}
        with ExitStack() as mem:
            phase_a(nc, ctx, mem, a, h_rows, n_rows, logits, progs)
        if upto >= "B":
            with ExitStack() as mem:
                progs["after_b"] = phase_b(nc, ctx, mem, a, h_rows, n_rows, logits, progs["after_a"], progs)
        if upto >= "C":
            with ExitStack() as mem:
                phase_c(nc, ctx, mem, a, h_rows, out, progs["after_b"], progs)
        if upto == "B":
            progs["z_sync"] = progs["after_b"]
        if upto == "A":
            progs["z_sync"] = progs["after_a"]

        @block.sync
        def _(sp):
            progs["a_sync"](sp)
            for part in ("b", "c", "z"):
                if part + "_sync" in progs:
                    progs[part + "_sync"](sp)

        @block.vector
        def _(dve):
            progs["a_vector"](dve)
            for part in ("b", "c", "z"):
                if part + "_vector" in progs:
                    progs[part + "_vector"](dve)

        @block.scalar
        def _(act):
            progs["a_scalar"](act)
            for part in ("b", "c", "z"):
                if part + "_scalar" in progs:
                    progs[part + "_scalar"](act)

        @block.gpsimd
        def _(pool):
            progs["a_gpsimd"](pool)
            for part in ("b", "c", "z"):
                if part + "_gpsimd" in progs:
                    progs[part + "_gpsimd"](pool)

        @block.tensor
        def _(pe):
            progs["a_tensor"](pe)
            for part in ("b", "c", "z"):
                if part + "_tensor" in progs:
                    progs[part + "_tensor"](pe)


def phase_a(nc, ctx, mem, a, h_rows, n_rows, logits, progs):
    def sb(name, shape, dt=F32):
        return mem.enter_context(nc.sbuf_tensor("a_" + name, shape, dt))

    def ps(name, shape, dt=F32):
        return mem.enter_context(nc.psum_tensor("a_" + name, shape, dt))

    def sem(name):
        return ctx.enter_context(nc.semaphore("a_" + name))

    wtok = sb("wtok", [PV, D])
    w_in = sb("w_in", [P, 2 * DI])
    w_bc = sb("w_bc", [P, 2, P])
    w_dt = sb("w_dt", [P, 2, DI])
    w_out = sb("w_out", [P, 2, D])
    w_r = sb("w_r", [P, E0])
    cols = sb("cols", [P, 49])
    btok, cls2, gain, bias = cols[:, 0:1], cols[:, 1:3], cols[:, 3:4], cols[:, 4:5]
    conv_b, dt_b, taps, log_a = cols[:, 5:7], cols[:, 7:9], cols[:, 9:17], cols[:, 17:49]
    neg_a = sb("neg_a", [P, 2 * NS])
    ident = sb("ident", [P, P])
    mean_w = sb("mean_w", [P, P])
    zero_rows = sb("zero_rows", [RB - T, D])
    least = sb("least", [E0, NLG - NTOK])
    eps_cols = sb("eps_cols", [P, 2])
    picks = sb("picks", [P, 2 * NS])
    sel = sb("sel", [P, 2 * NS, P], BF16)

    xp = [sb(f"xp{s}", [PV, W]) for s in range(2)]
    h0 = sb("h0", [P, W])
    xc = sb("xc", [P, W])
    sq = sb("sq", [P, W])
    r1 = sb("r1", [P, W])
    r12 = sb("r12", [P, W])
    l1, l12, l2 = sb("l1", [P, W]), sb("l12", [P, W]), sb("l2", [P, W])
    u = sb("u", [P, W])
    n1 = sb("n1", [P, W])
    xn = sb("xn", [P, W])
    xr = [sb(f"xr{s}", [P, 2, KC - 1 + W]) for s in range(2)]
    tail0 = sb("tail0", [P, 2, KC - 1])
    cv = sb("cv", [P, 2, W])
    xm = sb("xm", [P, 2, W])
    bcr = sb("bcr", [P, W])
    spx = sb("spx", [P, 2, W])
    spe = sb("spe", [P, 2, W])
    spl = sb("spl", [P, 2, W])
    yt = sb("yt", [P, 2, W])
    hn = [sb(f"hn{s}", [P, W]) for s in range(2)]
    sz = [sb(f"sz{s}", [P, 2, W]) for s in range(2)]
    dt = [sb(f"dt{s}", [P, 2, W]) for s in range(2)]
    dtx = [sb(f"dtx{s}", [P, 2, W]) for s in range(2)]
    bc = [sb(f"bc{s}", [P, W], BF16) for s in range(2)]
    da = sb("da", [P, DA_RING, W])
    dbx = sb("dbx", [P, 4, W])
    h = sb("h", [P, H_RING, W])
    hc = sb("hc", [P, HC_RING, W])
    cs = sb("cs", [P, CS_RING, W])
    carry = [sb(f"state{s}", [P, STEPS]) for s in range(2)]
    carry0 = sb("state_prefix", [P, STEPS])
    yz = sb("yz", [P, 2, W])
    h1 = sb("h1", [P, W])
    xc2 = sb("xc2", [P, W])
    sq2 = sb("sq2", [P, W])
    r2 = sb("r2", [P, W])
    n2 = sb("n2", [P, W])
    lg = sb("lg", [E0, W])
    th = sb("th", [TT, NT * D])
    tn = sb("tn", [TT, NT * D])

    b_bank = [ps(f"b_bank{i}", [P, 512]) for i in range(2)]
    c_bank = [ps(f"c_bank{i}", [P, 512]) for i in range(2)]
    y_bank = [ps(f"y_bank{i}", [P, 512]) for i in range(2)]
    work = [ps(f"work{i}", [P, 512]) for i in range(2)]

    s_weights = sem("weights")
    s_const, s_sel, s_neg_a = sem("const"), sem("sel"), sem("neg_a")
    s_patches = [sem(f"patches{s}") for s in range(2)]
    s_full = [sem(f"full{i}") for i in range(2)]
    s_free = [sem(f"free{i}") for i in range(2)]
    s_h0, s_sq, s_r1, s_u, s_n1, s_hn, s_xn = map(sem, ("h0", "sq", "r1", "u", "n1", "hn", "xn"))
    s_fresh = sem("fresh")
    s_l1, s_r12, s_r2 = map(sem, ("l1", "r12", "r2"))
    s_tap0, s_conv_step, s_conv, s_tail, s_xm = map(sem, ("tap0", "conv_step", "conv", "tail", "xm"))
    s_bch, s_bcm, s_bc = map(sem, ("bch", "bcm", "bc"))
    s_abs, s_spe, s_spl, s_spu, s_spd, s_spm, s_dt, s_dtx = map(
        sem, ("abs", "spe", "spl", "spu", "spd", "spm", "dt", "dtx"))
    s_b, s_c, s_cs, s_da, s_dbx, s_scan, s_carry, s_hc, s_sum = map(
        sem, ("b", "c", "cs", "da", "dbx", "scan", "carry", "hc", "sum"))
    s_reset = sem("reset")
    s_yz, s_sq2, s_n2 = map(sem, ("yz", "sq2", "n2"))
    s_again, s_end = sem("again"), sem("end")
    s_lg_out, s_th_out, s_tn_out = sem("lg_out"), sem("th_out"), sem("tn_out")
    N_WEIGHTS = 9

    def sync(sp):
        for dst, src in ((wtok[:], a["wtok"]), (cols[:], a["cols"]), (w_in[:], a["w_in"]), (ident[:], a["ident"]),
                         (picks[:], a["picks"]), (w_bc[:], a["w_bc"]), (w_dt[:], a["w_dt"]), (w_out[:], a["w_out"]),
                         (w_r[:], a["w_r"])):
            sp.dma_start(dst, src).then_inc(s_weights, 16)
        for t in phase_a_turns(sp):
            if t.pre and t.pre_w == W:
                image, c = t.pre_at
                p = t.q + 1
                if not (isinstance(t.q, int) and p <= 2):
                    need(sp, s_hn, p - 1)
                sp.dma_start(xp[t.slot ^ 1][:], a["patches"][:, ds(image * NPATCH + c * W, W)]).then_inc(s_patches[t.slot ^ 1], 16)
            if t.post and t.post_w == 2:
                for b in range(BATCH):
                    taken(sp, t, "logit")
                    sp.dma_start(logits[:, b * T:b * T + 2], lg[:, 0:2]).then_inc(s_lg_out, 16)
                for b in range(BATCH):
                    taken(sp, t, "trh")
                    sp.dma_start(h_rows[b * RB:b * RB + 2, :], th[0:2, 0:D]).then_inc(s_th_out, 16)
                for b in range(BATCH):
                    taken(sp, t, "trn")
                    sp.dma_start(n_rows[b * RB:b * RB + 2, :], tn[0:2, 0:D]).then_inc(s_tn_out, 16)
            elif t.post:
                image, c = t.post_at
                taken(sp, t, "logit")
                sp.dma_start(logits[:, ds(image * T + 2 + c * W, W)], lg[:]).then_inc(s_lg_out, 16)
                for use, tile, rows, done in (("trh", th, h_rows, s_th_out), ("trn", tn, n_rows, s_tn_out)):
                    taken(sp, t, use)
                    sp.dma_start(rows[ds(image * RB + 2 + c * W, W), :].rearrange("(j p) d -> p j d", p=TT),
                                 tile[:].rearrange("p (j d) -> p j d", j=NT)).then_inc(done, 16)
        outs = BATCH + 2 * NCH * (BATCH // 2)
        for done in (s_lg_out, s_th_out, s_tn_out):
            sp.wait_ge(done, 16 * outs)
        for b in range(BATCH):
            for rows in (h_rows, n_rows):
                sp.dma_start(rows[b * RB + T:b * RB + T + SHIFT, :], rows[b * RB:b * RB + SHIFT, :]
                             ).then_inc(s_again, 16)
        sp.wait_ge(s_again, 16 * 2 * BATCH)
        for rows in (h_rows, n_rows):
            for b in range(BATCH):
                sp.dma_start(rows[b * RB + T + SHIFT:(b + 1) * RB + SHIFT, :], zero_rows[:]).then_inc(s_end, 16)
            sp.dma_start(rows[0:SHIFT, :], zero_rows[0:SHIFT, :]).then_inc(s_end, 16)
        sp.dma_start(logits[:, NTOK:NLG], least[:]).then_inc(s_end, 16)

    def bank(t, use):
        return work[t.bank_of(use)]

    def result(eng, t, use):
        eng.wait_ge(s_full[t.bank_of(use)], t.nth(use) + 1)
        return s_free[t.bank_of(use)]

    def taken(eng, t, use):
        eng.wait_ge(s_free[t.bank_of(use)], t.nth(use) + 1)

    def h0_ready(eng, t):
        if t.pre_w == W:
            taken(eng, t, "tok")
        else:
            eng.wait_ge(s_h0, 1)

    def tensor(pe):
        def begin(t, use):
            need(pe, s_free[t.bank_of(use)], t.nth(use))
            return bank(t, use)

        def end(t, use, mm):
            mm.then_inc(s_full[t.bank_of(use)], 1)

        def spread(q, slot, n, w):
            if n == 0:
                pe.wait_ge(s_bc, q + 1)
            need(pe, s_dbx, q * STEPS + 2 * n - 2)
            pe.matmul(b_bank[n % 2][:, 0:w], sel[:, n, :], bc[slot][:, 0:w], start=True, stop=True).then_inc(s_b, 1)
            need(pe, s_cs, q * NS + n - 1)
            pe.matmul(c_bank[n % 2][:, 0:w], sel[:, NS + n, :], bc[slot][:, 0:w], start=True, stop=True).then_inc(s_c, 1)

        def add(t, k):
            n, d = divmod(k, 2)
            if n == 0:
                need(pe, s_yz, t.q * 2)
            pe.wait_ge(s_hc, t.q * STEPS + (k + 1))
            pe.matmul(y_bank[d][:, 0:t.w], ident[:], hc[:, k % HC_RING, 0:t.w], start=(n == 0), stop=(n == NS - 1)
                      ).then_inc(s_sum, 1)

        pe.wait_ge(s_weights, 16 * N_WEIGHTS)
        pe.wait_ge(s_const, 1)
        pe.wait_ge(s_sel, 1)
        for t in phase_a_turns(pe):
            p, pw = t.q + 1, t.pre_w
            rw, so = t.post_w, t.slot ^ 1
            for k in range(STEPS):
                if t.scan and k % 2 == 1:
                    n = (k - 1) // 2 + 2
                    if n < NS:
                        spread(t.q, t.slot, n, t.w)
                if t.scan and k >= SUM_LAG:
                    add(t, k - SUM_LAG)
                if t.pre:
                    if k == 1 and pw == W:
                        o = begin(t, "tok")
                        pe.wait_ge(s_patches[so], (t.pre_at[0] // 2 * NCH + 1 + t.pre_at[1]) * 16)
                        end(t, "tok", pe.matmul(o[:, 0:pw], wtok[:], xp[so][:], start=True, stop=True))
                    if k == 3:
                        o = begin(t, "mean")
                        h0_ready(pe, t)
                        end(t, "mean", pe.matmul(o[:, 0:pw], mean_w[:], h0[:, 0:pw], start=True, stop=True))
                    if k == 6:
                        o = begin(t, "var")
                        pe.wait_ge(s_sq, p + 1)
                        end(t, "var", pe.matmul(o[:, 0:pw], mean_w[:], sq[:, 0:pw], start=True, stop=True))
                    for use, at, m in (("xm0", 10, 0), ("xm1", 10, 1), ("z0", 13, 2), ("z1", 15, 3)):
                        if k == at:
                            o = begin(t, use)
                            pe.wait_ge(s_xn, p + 1)
                            end(t, use, pe.matmul(o[:, 0:pw], w_in[:, m * P:(m + 1) * P], xn[:, 0:pw], start=True,
                                                  stop=True))
                    if k == 17:
                        o = begin(t, "bc")
                        pe.wait_ge(s_xm, p + 1)
                        for j in range(2):
                            mm = pe.matmul(o[:, 0:pw], w_bc[:, j, :], xm[:, j, 0:pw], start=(j == 0), stop=(j == 1))
                        end(t, "bc", mm)
                    for use, at, m in (("dt0", 18, 0), ("dt1", 20, 1)):
                        if k == at:
                            o = begin(t, use)
                            for j in range(2):
                                mm = pe.matmul(o[:, 0:pw], w_dt[:, j, m * P:(m + 1) * P], xm[:, j, 0:pw],
                                               start=(j == 0), stop=(j == 1))
                            end(t, use, mm)
                if t.post:
                    if k == 5:
                        o = begin(t, "out")
                        pe.wait_ge(s_yz, t.q * 2)
                        pe.wait_ge(s_hn, t.q)
                        for j in range(2):
                            pe.matmul(o[:, 0:rw], w_out[:, j, :], yz[:, j, 0:rw], start=(j == 0), stop=False)
                        end(t, "out", pe.matmul(o[:, 0:rw], ident[:], hn[so][:, 0:rw], start=False, stop=True))
                    if k == 9:
                        o = begin(t, "mean2")
                        taken(pe, t, "out")
                        end(t, "mean2", pe.matmul(o[:, 0:rw], mean_w[:], h1[:, 0:rw], start=True, stop=True))
                    if k == 12:
                        o = begin(t, "var2")
                        pe.wait_ge(s_sq2, t.q)
                        end(t, "var2", pe.matmul(o[:, 0:rw], mean_w[:], sq2[:, 0:rw], start=True, stop=True))
                    if k == 16:
                        o = begin(t, "logit")
                        pe.wait_ge(s_n2, t.q)
                        end(t, "logit", pe.matmul(o[0:E0, 0:rw], w_r[:], n2[:, 0:rw], start=True, stop=True))
                    for use, at, src in (("trh", 22, h1), ("trn", 24, n2)):
                        if k == at:
                            o = begin(t, use)
                            tiles = NT if rw == W else 1
                            m = min(rw, TT)
                            for j in range(tiles):
                                mm = pe.transpose(o[0:m, j * D:(j + 1) * D], src[:, j * TT:j * TT + m], ident[:])
                            end(t, use, mm)
            if t.pre:
                for n in range(2):
                    spread(p, so, n, pw)
            if t.scan:
                for k in range(STEPS - SUM_LAG, STEPS):
                    add(t, k)

    def scalar(act):
        act.wait_ge(s_weights, 16 * N_WEIGHTS)
        act.wait_ge(s_const, 1)
        act.preload_act_table_set("natural_log_exp_and_others")
        act.activation(neg_a[:], log_a, ACT.Exp).then_inc(s_neg_a, 1)
        for t in phase_a_turns(act):
            p, pw, so = t.q + 1, t.pre_w, t.slot ^ 1
            rw = t.post_w
            for k in range(STEPS):
                if t.scan:
                    n, d = divmod(k, 2)
                    if k == 0:
                        act.wait_ge(s_dt, t.q + 1)
                        act.wait_ge(s_neg_a, 2)
                    need(act, s_scan, t.q * STEPS + (k + 1 - DA_RING))
                    act.activation(da[:, k % DA_RING, 0:t.w], dt[t.slot][:, d, 0:t.w], ACT.Exp,
                                   scale=neg_a[:, d * NS + n:d * NS + n + 1]).then_inc(s_da, 1)
                    if d == 0:
                        act.wait_ge(s_c, t.q * NS + (n + 1))
                        need(act, s_hc, t.q * STEPS + 2 * (n - CS_RING) + 2)
                        act.copy(cs[:, n % CS_RING, 0:t.w], c_bank[n % 2][:, 0:t.w]).then_inc(s_cs, 1)
                if t.pre:
                    if k == 2:
                        need(act, s_hn, p)
                        if pw == W:
                            free = result(act, t, "tok")
                            act.activation(h0[:, 0:pw], bank(t, "tok")[:, 0:pw], ACT.Identity, bias=btok
                                           ).then_inc(free, 1)
                        else:
                            act.copy(h0[:, 0:2], cls2).then_inc(s_h0, 1)
                    if k == 5:
                        taken(act, t, "mean")
                        act.activation(sq[:, 0:pw], xc[:, 0:pw], ACT.Square).then_inc(s_sq, 1)
                    if k == 7:
                        free = result(act, t, "var")
                        v = bank(t, "var")[:, 0:pw]
                        act.activation(l1[:, 0:pw], v, ACT.Ln, bias=eps_cols[:, 0:1]).then_inc(s_l1, 1)
                        act.activation(l12[:, 0:pw], v, ACT.Ln, bias=eps_cols[:, 1:2]).then_inc(free, 1)
                        act.wait_ge(s_l1, p + 1)
                        need(act, s_n1, p)
                        act.activation(r1[:, 0:pw], l1[:, 0:pw], ACT.Exp, scale=-0.5).then_inc(s_r1, 1)
                        taken(act, t, "var")
                        act.activation(r12[:, 0:pw], l12[:, 0:pw], ACT.Exp, scale=-0.5).then_inc(s_r12, 1)
                    if k == 9:
                        act.wait_ge(s_u, p + 1)
                        act.activation(xn[:, 0:pw], u[:, 0:pw], ACT.Identity, scale=gain, bias=bias).then_inc(s_xn, 1)
                    if k == 11:
                        for d, use in enumerate(("xm0", "xm1")):
                            free = result(act, t, use)
                            act.copy(xr[so][:, d, KC - 1:KC - 1 + pw], bank(t, use)[:, 0:pw]).then_inc(free, 1)
                        for d, use in enumerate(("xm0", "xm1")):
                            taken(act, t, use)
                            act.activation(cv[:, d, 0:pw], xr[so][:, d, KC - 1:KC - 1 + pw], ACT.Identity,
                                           scale=taps[:, d * KC + KC - 1:d * KC + KC], bias=conv_b[:, d:d + 1]
                                           ).then_inc(s_tap0, 1)
                    if k == 16:
                        for d, use in enumerate(("z0", "z1")):
                            free = result(act, t, use)
                            act.activation(sz[so][:, d, 0:pw], bank(t, use)[:, 0:pw], ACT.Silu).then_inc(free, 1)
                        act.wait_ge(s_conv, (p + 1) * 2)
                        need(act, s_dtx, p)
                        act.activation(xm[:, :, 0:pw], cv[:, :, 0:pw], ACT.Silu).then_inc(s_xm, 1)
                        act.preload_act_table_set("natural_log_exp_and_others")
                    if k == 18:
                        act.wait_ge(s_full[t.bank_of("bc")], t.nth("bc") + 1)
                        act.copy(bc[so][:, 0:pw], bank(t, "bc")[:, 0:pw]).then_inc(s_bch, 1)
                    if k == 20:
                        taken(act, t, "bc")
                        act.copy(bc[so][64:128, 0:pw], bcr[64:128, 0:pw]).then_inc(s_bcm, 1)
                    if k == 19 or k == 22:
                        d = int(k == 22)
                        free = result(act, t, f"dt{d}")
                        need(act, s_dt, p)
                        act.activation(spx[:, d, 0:pw], bank(t, f"dt{d}")[:, 0:pw], ACT.Identity,
                                       bias=dt_b[:, d:d + 1]).then_inc(free, 1)
                    if k == 23:
                        for d in range(2):
                            taken(act, t, f"dt{d}")
                        act.activation(spe[:, :, 0:pw], spx[:, :, 0:pw], ACT.Abs).then_inc(s_abs, 1)
                        act.wait_ge(s_abs, p + 1)
                        act.activation(spe[:, :, 0:pw], spe[:, :, 0:pw], ACT.Exp, scale=-1.0).then_inc(s_spe, 1)
                        act.wait_ge(s_spe, p + 1)
                        act.activation(spl[:, :, 0:pw], spe[:, :, 0:pw], ACT.Ln, bias=1.0).then_inc(s_spl, 1)
                if t.post:
                    if k == 8:
                        free = result(act, t, "out")
                        act.copy(h1[:, 0:rw], bank(t, "out")[:, 0:rw]).then_inc(free, 1)
                    if k == 11:
                        taken(act, t, "mean2")
                        act.activation(sq2[:, 0:rw], xc2[:, 0:rw], ACT.Square).then_inc(s_sq2, 1)
                    if k == 14:
                        free = result(act, t, "var2")
                        act.activation(l2[:, 0:rw], bank(t, "var2")[:, 0:rw], ACT.Ln, bias=eps_cols[:, 0:1]
                                       ).then_inc(free, 1)
                        taken(act, t, "var2")
                        act.activation(r2[:, 0:rw], l2[:, 0:rw], ACT.Exp, scale=-0.5).then_inc(s_r2, 1)
                    outs = 0 if rw == 2 else 16 * (BATCH - 2)
                    for use, at, dst, done in (("logit", 17, lg, s_lg_out), ("trh", 23, th, s_th_out),
                                               ("trn", 25, tn, s_tn_out)):
                        if k == at:
                            free = result(act, t, use)
                            if rw == W:
                                need(act, done, t.q * 16 + outs)
                            m, cols_ = (E0, rw) if use == "logit" else (min(rw, TT), NT * D if rw == W else D)
                            act.copy(dst[0:m, 0:cols_], bank(t, use)[0:m, 0:cols_]).then_inc(free, 1)

    def vector(dve):
        dve.memset(mean_w[:], 1.0 / D)
        dve.memset(zero_rows[:], 0.0)
        dve.memset(least[:], -3.0e38)
        dve.memset(eps_cols[:, 0:1], EPS)
        dve.memset(eps_cols[:, 1:2], EPS * EPS / (1 + EPS))
        for s in range(2):
            dve.memset(xr[s][:, :, 0:KC - 1], 0.0)
        dve.memset(carry0[:], 0.0).then_inc(s_const, 1)
        dve.wait_ge(s_const, 1)
        dve.wait_ge(s_weights, 16 * N_WEIGHTS)
        for j in range(2 * NS):
            i = dve.tensor_copy(sel[:, j, :], picks[:, j:j + 1].to_broadcast([P, P]))
        i.then_inc(s_sel, 1)
        dve.wait_ge(s_neg_a, 1)
        dve.tensor_scalar(neg_a[:], neg_a[:], -1.0, None, ALU.mult).then_inc(s_neg_a, 1)
        resets = pairs = 0
        for t in phase_a_turns(dve):
            p, pw, so = t.q + 1, t.pre_w, t.slot ^ 1
            rw, w = t.post_w, t.w
            states = carry0 if t.first else carry[t.slot]

            def keep(k):
                dve.wait_ge(s_scan, t.q * STEPS + (k + 1))
                first = k + 1 - 8
                dve.tensor_copy(states[:, first:k + 1],
                                h[:, first % H_RING:first % H_RING + 8, w - 1:w].rearrange("p k o -> p (k o)")
                                ).then_inc(s_carry, 1)

            for k in range(STEPS + 1):
                if t.scan:
                    if k < STEPS:
                        n, d = divmod(k, 2)
                        if k == 0:
                            dve.wait_ge(s_dtx, t.q + 1)
                        dve.wait_ge(s_b, t.q * NS + (n + 1))
                        need(dve, s_scan, t.q * STEPS + (k - 3))
                        dve.tensor_tensor(dbx[:, k % 4, 0:w], dtx[t.slot][:, d, 0:w], b_bank[n % 2][:, 0:w], ALU.mult
                                          ).then_inc(s_dbx, 1)
                    if k > 0:
                        j = k - 1
                        if j == 0:
                            need(dve, s_carry, t.q * 4 - 4)
                        dve.wait_ge(s_da, t.q * STEPS + (j + 1))
                        dve.wait_ge(s_dbx, t.q * STEPS + (j + 1))
                        need(dve, s_hc, t.q * STEPS + (j + 1 - H_RING))
                        n, d = divmod(j, 2)
                        dve.tensor_tensor_scan(h[:, j % H_RING, 0:w], da[:, j % DA_RING, 0:w], dbx[:, j % 4, 0:w],
                                               0.0 if t.first else states[:, j:j + 1], ALU.mult, ALU.add
                                               ).then_inc(s_scan, 1)
                        if k > 8 and (k - 1) % 8 == 0:
                            keep(k - 2)
                if t.post:
                    if k == 4:
                        dve.wait_ge(s_sum, t.q * STEPS)
                        for d in range(2):
                            dve.tensor_tensor(yz[:, d, 0:rw], sz[so][:, d, 0:rw], y_bank[d][:, 0:rw], ALU.mult
                                              ).then_inc(s_yz, 1)
                    if k == 10:
                        free = result(dve, t, "mean2")
                        dve.tensor_tensor(xc2[:, 0:rw], h1[:, 0:rw], bank(t, "mean2")[:, 0:rw], ALU.subtract
                                          ).then_inc(free, 1)
                    if k == 15:
                        dve.wait_ge(s_r2, t.q)
                        dve.tensor_tensor(n2[:, 0:rw], xc2[:, 0:rw], r2[:, 0:rw], ALU.mult).then_inc(s_n2, 1)
                if t.pre:
                    if k == 4:
                        free = result(dve, t, "mean")
                        need(dve, s_n1, p)
                        dve.tensor_tensor(xc[:, 0:pw], h0[:, 0:pw], bank(t, "mean")[:, 0:pw], ALU.subtract
                                          ).then_inc(free, 1)
                    if k == 8:
                        dve.wait_ge(s_r12, p + 1)
                        dve.scalar_tensor_tensor(out=u[:, 0:pw], in0=xc[:, 0:pw], scalar=(1 + EPS) ** -0.5,
                                                 in1=r12[:, 0:pw], op0=ALU.mult, op1=ALU.mult).then_inc(s_u, 1)
                    if k == 11 and t.fresh:
                        pairs += 1
                        need(dve, s_tail, p)
                        for s in range(2):
                            dve.tensor_copy(xr[s][:, :, 0:KC - 1], tail0[:]).then_inc(s_fresh, 1)
                        dve.wait_ge(s_fresh, 2 * pairs)
                    if k in (12, 13, 14):
                        for d in range(2):
                            if k == 12 and d == 0:
                                need(dve, s_tail, p)
                            if k == 12:
                                dve.wait_ge(s_tap0, p * 2 + (d + 1))
                            else:
                                dve.wait_ge(s_conv_step, p * 4 + (2 * (k - 13) + d + 1))
                            j = 14 - k
                            i = dve.scalar_tensor_tensor(
                                out=cv[:, d, 0:pw], in0=xr[so][:, d, j:j + pw], scalar=taps[:, d * KC + j:d * KC + j + 1],
                                in1=cv[:, d, 0:pw], op0=ALU.mult, op1=ALU.add)
                            i.then_inc(s_conv if k == 14 else s_conv_step, 1)
                    if k == 15:
                        dve.wait_ge(s_conv, (p + 1) * 2)
                        dst = tail0[:] if pw == 2 else xr[so][:, :, 0:KC - 1]
                        dve.tensor_copy(dst, xr[so][:, :, pw:pw + KC - 1]).then_inc(s_tail, 1)
                    if k == 19:
                        dve.wait_ge(s_bch, p + 1)
                        dve.tensor_tensor(bcr[64:128, 0:pw], bank(t, "bc")[64:128, 0:pw], bc[so][64:128, 0:pw],
                                          ALU.subtract).then_inc(s_free[t.bank_of("bc")], 1)
                    if k == 21:
                        dve.wait_ge(s_bcm, p + 1)
                        dve.tensor_tensor(bc[so][96:128, 0:pw], bcr[96:128, 0:pw], bc[so][96:128, 0:pw],
                                          ALU.subtract).then_inc(s_bc, 1)
                    if k == 24:
                        dve.wait_ge(s_spe, p + 1)
                        need(dve, s_spm, p)
                        dve.tensor_scalar(yt[:, :, 0:pw], spe[:, :, 0:pw], 1.0, None, ALU.add).then_inc(s_spu, 1)
                        dve.wait_ge(s_spu, p + 1)
                        dve.scalar_tensor_tensor(out=yt[:, :, 0:pw], in0=yt[:, :, 0:pw], scalar=-1.0,
                                                 in1=spe[:, :, 0:pw], op0=ALU.add, op1=ALU.subtract).then_inc(s_spd, 1)
                    if k == 27:
                        dve.wait_ge(s_spm, p + 1)
                        dve.scalar_tensor_tensor(out=dt[so][:, :, 0:pw], in0=spx[:, :, 0:pw], scalar=0.0,
                                                 in1=spl[:, :, 0:pw], op0=ALU.max, op1=ALU.add).then_inc(s_dt, 1)
            if t.scan:
                keep(STEPS - 1)
            if t.first or t.reset:
                dve.wait_ge(s_carry, 4 * (t.q + 1))
                for s in range(2):
                    dve.tensor_copy(carry[s][:], carry0[:]).then_inc(s_reset, 1)
                resets += 2
                dve.wait_ge(s_reset, resets)

    def gpsimd(pool):
        for t in phase_a_turns(pool):
            p, pw, so = t.q + 1, t.pre_w, t.slot ^ 1
            for k in range(STEPS):
                if t.scan:
                    n, d = divmod(k, 2)
                    pool.wait_ge(s_scan, t.q * STEPS + (k + 1))
                    if d == 0:
                        pool.wait_ge(s_cs, t.q * NS + (n + 1))
                    need(pool, s_sum, t.q * STEPS + (k + 1 - HC_RING))
                    pool.tensor_tensor(hc[:, k % HC_RING, 0:t.w], h[:, k % H_RING, 0:t.w],
                                       cs[:, n % CS_RING, 0:t.w], ALU.mult).then_inc(s_hc, 1)
                if t.pre:
                    if k == 8:
                        pool.wait_ge(s_r1, p + 1)
                        pool.tensor_tensor(n1[:, 0:pw], xc[:, 0:pw], r1[:, 0:pw], ALU.mult).then_inc(s_n1, 1)
                    if k == 9:
                        pool.wait_ge(s_n1, p + 1)
                        pool.tensor_tensor(hn[so][:, 0:pw], h0[:, 0:pw], n1[:, 0:pw], ALU.add).then_inc(s_hn, 1)
                    if k == 25:
                        pool.wait_ge(s_spd, p + 1)
                        pool.wait_ge(s_spl, p + 1)
                        pool.tensor_tensor(spl[:, :, 0:pw], spl[:, :, 0:pw], yt[:, :, 0:pw], ALU.subtract
                                           ).then_inc(s_spm, 1)
                    if k == 28:
                        pool.wait_ge(s_dt, p + 1)
                        pool.tensor_tensor(dtx[so][:, :, 0:pw], dt[so][:, :, 0:pw], xm[:, :, 0:pw], ALU.mult
                                           ).then_inc(s_dtx, 1)

    progs.update(after_a=lambda eng: eng.wait_ge(s_end, 16 * (2 * BATCH + 3)), a_sync=sync, a_scalar=scalar, a_vector=vector, a_gpsimd=gpsimd, a_tensor=tensor)


def phase_b(nc, ctx, mem, a, h_rows, n_rows, logits, after_a, progs):
    def sb(name, shape, dt=F32):
        return mem.enter_context(nc.sbuf_tensor("b_" + name, shape, dt))

    def ps(name, shape, dt=F32):
        return mem.enter_context(nc.psum_tensor("b_" + name, shape, dt))

    def sem(name):
        return ctx.enter_context(nc.semaphore("b_" + name))

    TILES = CAP // P
    FT = FF // P
    ROW_BITS = 14
    MOVE_BITS = 11
    WIDE = CAP + SPAN

    x = sb("x", [P, SPAN])
    tmp = sb("tmp", [P, SPAN])
    tmp_a = sb("tmp_a", [P, SPAN])
    ones = sb("ones", [P, SPAN])
    gt = sb("gt", [P, SPAN])
    eq = sb("eq", [P, SPAN])
    rank = sb("rank", [P, SPAN])
    place = sb("place", [P, SPAN])
    iota = sb("iota", [P, SPAN])
    rows = sb("rows", [P, SPAN], I32)
    chosen = sb("chosen", [P, SPAN], I32)
    entry = sb("entry", [P, SPAN], I32)
    lists = [sb(f"lists{i}", [P, WIDE], I32) for i in range(2)]
    moves = sb("moves", [P, WIDE], I32)
    zeros = sb("zeros", [P, WIDE], I32)
    listf = sb("listf", [P, CAP])
    group = sb("group", [P, P])
    before = sb("before", [P, P])
    first = sb("first", [P, E0])
    member = sb("member", [P, E0])
    ident = sb("ident", [P, P])
    small = sb("small", [P, 16])
    smalli = sb("smalli", [P, 8], I32)
    row = sb("row", [1, P])
    row8 = sb("row8", [1, E0])
    wide_col = sb("wide_col", [P, 2, P])
    index = sb("index", [P, TILES, E0], U32)
    tab = sb("tab", [P, 3, E0])
    w1 = [sb(f"w1{s}", [P, FF]) for s in range(2)]
    w2 = [sb(f"w2{s}", [P, FT, D]) for s in range(2)]
    b1 = [sb(f"b1{s}", [P, FT]) for s in range(2)]
    b2 = [sb(f"b2{s}", [1, D]) for s in range(2)]
    mine = [sb(f"mine{s}", [P, 3]) for s in range(2)]
    idx = [sb(f"idx{s}", [P, TILES], U32) for s in range(2)]
    xg = [[sb(f"xg{s}_{i}", [P, D]) for i in range(TILES)] for s in range(2)]
    xt = [sb(f"xt{s}", [P, CAP]) for s in range(2)]
    hid = sb("hid", [P, FT, CAP])
    wexp = [sb(f"wexp{s}", [P, TILES]) for s in range(2)]
    og = [[sb(f"og{s}_{i}", [P, D]) for i in range(TILES)] for s in range(2)]

    p_small = ps("p_small", [P, 512])
    p_tr = [ps(f"p_tr{i}", [P, 512]) for i in range(2)]
    p_h = [ps(f"p_h{i}", [P, 512]) for i in range(2)]
    p_o = [ps(f"p_o{i}", [P, 512]) for i in range(2)]
    p_l = ps("p_l", [P, 512])

    s_in, s_dve, s_pe, s_act = sem("in"), sem("dve"), sem("pe"), sem("act")
    s_w = [sem(f"w{s}") for s in range(2)]
    s_lists, s_index = sem("lists"), sem("index")
    s_mine, s_gather, s_tr, s_xt, s_logit, s_wexp, s_hid_mm, s_hid, s_out_mm, s_og, s_scatter = (
        sem("mine"), [sem(f"gather{s}") for s in range(2)], sem("tr"), sem("xt"), sem("logit"), sem("wexp"),
        sem("hid_mm"), sem("hid"), sem("out_mm"), sem("og"), sem("scatter"))
    LOADS = 8
    TAB = 10

    def sync(sp):
        after_a(sp)
        for dst, src in ((x[:], logits.rearrange("e (s j) -> (e s) j", s=16)), (rows[:], a["rows"]),
                         (iota[:], a["iota"]), (group[:], a["group"]), (before[:], a["before"]),
                         (first[:], a["first"]), (member[:], a["member"]), (ident[:], a["ident"])):
            sp.dma_start(dst, src).then_inc(s_in, 16)
        sp.dma_start(tab[:, 0, 0:E0], a["w_r"]).then_inc(s_in, 16)
        with sp.Fori(0, E0 // 2) as j:
            for s in range(2):
                e = j * 2 + s
                sp.wait_ge(s_out_mm, e * TILES + TILES)
                sp.dma_start(w1[s][:], a["w1"][ds(e * P, P), :]).then_inc(s_w[s], 16)
                sp.dma_start(w2[s][:].rearrange("p f d -> p (f d)"), a["w2"][ds(e * P, P), :]).then_inc(s_w[s], 16)
                sp.dma_start(b1[s][:], a["b1"][ds(e * P, P), :]).then_inc(s_w[s], 16)
                sp.dma_start(b2[s][:], a["b2"][ds(e, 1), :]).then_inc(s_w[s], 16)

    def vector(dve):
        after_a(dve)
        count = [0]

        def do(i):
            count[0] += 1
            i.then_inc(s_dve, 1)
            dve.wait_ge(s_dve, count[0])

        dve.memset(small[:, 11:12], 0.0).then_inc(s_out_mm, 2 * TILES)
        dve.memset(small[:, 12:13], 0.0).then_inc(s_hid, 2)
        dve.memset(small[:, 13:14], 0.0).then_inc(s_og, 2)
        do(dve.memset(ones[:], 1.0))
        do(dve.memset(zeros[:], 0))
        do(dve.memset(lists[0][:], 0))
        dve.wait_ge(s_in, 16 * (LOADS + 1))
        do(dve.tensor_reduce(small[:, 0:1], x[:], AX.X, ALU.max))
        progs["n_rowmax"] = count[0]
        dve.wait_ge(s_pe, 1)
        do(dve.tensor_reduce(row8[:], p_small[0:1, 0:P].rearrange("o (e s) -> o e s", e=E0), AX.X, ALU.max))
        do(dve.tensor_copy(row[:].rearrange("o (e s) -> o e s", e=E0),
                           row8[:].unsqueeze(2).to_broadcast([1, E0, 16])))
        progs["n_row"] = count[0]
        dve.wait_ge(s_pe, 2)
        do(dve.tensor_scalar(small[:, 1:2], p_small[:, 128:129], -1.0, None, ALU.mult))
        progs["n_negmax"] = count[0]
        do(dve.tensor_scalar(tmp[:], x[:], 0.0, 0.0, ALU.is_ge, ALU.add, accum_out=small[:, 3:4]))
        progs["n_count0"] = count[0]
        dve.wait_ge(s_pe, 3)
        do(dve.tensor_scalar(small[:, 6:7], p_small[:, 129:130], float(CAP), None, ALU.is_ge))
        do(dve.tensor_scalar(smalli[:, 0:1], small[:, 6:7], -1.0, None, ALU.add))
        do(dve.memset(smalli[:, 1:2], 0))
        do(dve.memset(smalli[:, 2:3], 1 << 30))
        base = count[0]
        progs["n_search"] = base
        STEP = 8
        with dve.Fori(0, 31) as r:
            def step(n, i):
                i.then_inc(s_dve, 1)
                dve.wait_ge(s_dve, r * STEP + (base + n))
            step(1, dve.tensor_tensor(smalli[:, 3:4], smalli[:, 1:2], smalli[:, 2:3], ALU.bitwise_or))
            step(2, dve.tensor_tensor(smalli[:, 4:5], smalli[:, 3:4], smalli[:, 0:1], ALU.bitwise_xor))
            step(3, dve.tensor_scalar(tmp[:], x[:], smalli[:, 4:5].bitcast(F32), 0.0, ALU.is_ge, ALU.add,
                                      accum_out=small[:, 3:4]))
            dve.wait_ge(s_pe, r + 4)
            step(4, dve.tensor_scalar(small[:, 7:8], p_small[:, 129:130], float(CAP), None, ALU.is_ge))
            step(5, dve.tensor_scalar(smalli[:, 5:6], small[:, 7:8], -1.0, None, ALU.mult))
            step(6, dve.tensor_tensor(smalli[:, 6:7], smalli[:, 2:3], smalli[:, 5:6], ALU.bitwise_and))
            step(7, dve.tensor_tensor(smalli[:, 1:2], smalli[:, 1:2], smalli[:, 6:7], ALU.bitwise_or))
            step(8, dve.tensor_scalar(smalli[:, 2:3], smalli[:, 2:3], 1, None, ALU.logical_shift_right))
        count[0] = base + 31 * STEP
        do(dve.tensor_tensor(smalli[:, 4:5], smalli[:, 1:2], smalli[:, 0:1], ALU.bitwise_xor))
        thr = smalli[:, 4:5].bitcast(F32)
        do(dve.tensor_scalar(gt[:], x[:], thr, 0.0, ALU.is_gt, ALU.add, accum_out=small[:, 3:4]))
        do(dve.tensor_scalar(eq[:], x[:], thr, None, ALU.is_equal))
        do(dve.tensor_tensor_scan(rank[:], ones[:], eq[:], 0.0, ALU.mult, ALU.add))
        do(dve.tensor_copy(small[:, 4:5], rank[:, SPAN - 1:SPAN]))
        progs["n_eq"] = count[0]
        dve.wait_ge(s_pe, 36)
        do(dve.tensor_copy(small[:, 8:9], p_small[:, 129:130]))
        do(dve.tensor_tensor(small[:, 9:10], p_small[:, 130:131], small[:, 8:9], ALU.add))
        do(dve.tensor_scalar(rank[:], rank[:], small[:, 9:10], float(CAP), ALU.add, ALU.is_le))
        do(dve.tensor_tensor(eq[:], eq[:], rank[:], ALU.mult))
        do(dve.tensor_tensor(gt[:], gt[:], eq[:], ALU.add))
        do(dve.tensor_copy(chosen[:], gt[:]))
        do(dve.tensor_tensor_scan(rank[:], ones[:], gt[:], 0.0, ALU.mult, ALU.add))
        do(dve.tensor_copy(small[:, 5:6], rank[:, SPAN - 1:SPAN]))
        progs["n_sel"] = count[0]
        dve.wait_ge(s_pe, 38)
        do(dve.tensor_scalar(place[:], rank[:], p_small[:, 131:132], None, ALU.add))
        do(dve.tensor_tensor(place[:], iota[:], place[:], ALU.subtract))
        do(dve.tensor_copy(entry[:], place[:]))
        do(dve.tensor_scalar(entry[:], entry[:], ROW_BITS, None, ALU.logical_shift_left))
        do(dve.tensor_tensor(entry[:], entry[:], rows[:], ALU.bitwise_or))
        do(dve.copy_predicated(lists[0][:, CAP:WIDE], chosen[:], entry[:]))
        for b in range(MOVE_BITS):
            step_ = 1 << b
            lo = max(0, CAP - 2 * step_ + 1)
            cur, new = lists[b % 2], lists[(b + 1) % 2]
            do(dve.tensor_scalar(moves[:, lo:WIDE], cur[:, lo:WIDE], ROW_BITS + b, 1, ALU.logical_shift_right,
                                 ALU.bitwise_and))
            do(dve.tensor_copy(new[:, lo:WIDE], cur[:, lo:WIDE]))
            if b == 0:
                do(dve.memset(lists[1][:, 0:lo], 0))
            do(dve.copy_predicated(new[:, lo:WIDE], moves[:, lo:WIDE], zeros[:, lo:WIDE]))
            do(dve.copy_predicated(new[:, lo:WIDE - step_], moves[:, lo + step_:WIDE], cur[:, lo + step_:WIDE]))
        last = lists[MOVE_BITS % 2]
        do(dve.tensor_scalar(moves[:, 0:CAP], last[:, 0:CAP], (1 << ROW_BITS) - 1, None, ALU.bitwise_and))
        do(dve.tensor_copy(listf[:], moves[:, 0:CAP]))
        progs["n_list"] = count[0]
        do(dve.reciprocal(small[:, 10:11], p_small[:, 132:133]))
        for j, c in enumerate((1, 10)):
            do(dve.tensor_copy(wide_col[:, j, :], small[:, c:c + 1].to_broadcast([P, P])))
        progs["n_wide"] = count[0]
        dve.wait_ge(s_pe, 39)
        do(dve.tensor_copy(tab[:, 1:3, 0:E0], p_small[:, 256:256 + 2 * E0].rearrange("p (j e) -> p j e", j=2)))
        do(dve.tensor_copy(index[:], p_small[:, 192:192 + TILES * E0].rearrange("p (i e) -> p i e", e=E0)))

        def own_columns(e, s):
            need(dve, s_scatter, (e - 1) * 16 * TILES)
            dve.tensor_copy(mine[s][:], tab[:, :, e:e + 1].rearrange("p j o -> p (j o)")).then_inc(s_mine, 1)
            dve.tensor_copy(idx[s][:], index[:, :, e:e + 1].rearrange("p i o -> p (i o)")).then_inc(s_mine, 1)

        own_columns(0, 0)
        for e in range(E0):
            s = e % 2
            if e + 1 < E0:
                own_columns(e + 1, 1 - s)
            for half in range(2):
                dve.wait_ge(s_tr, e * 2 + (half + 1))
                dve.tensor_copy(xt[s][:, half * 512:half * 512 + 512], p_tr[half][:]).then_inc(s_xt, 1)
            dve.wait_ge(s_wexp, e + 1)
            for i in range(TILES):
                dve.wait_ge(s_out_mm, e * TILES + (2 * TILES + i + 1))
                dve.tensor_scalar(og[s][i][:], p_o[i % 2][:, 0:D], wexp[s][:, i:i + 1], mine[s][:, 2:3],
                                  ALU.mult, ALU.mult).then_inc(s_og, 1)

    def scalar(act):
        act.wait_ge(s_dve, progs["n_negmax"])
        act.activation(tmp_a[:], x[:], ACT.Exp, bias=small[:, 1:2], accum_out=small[:, 2:3]).then_inc(s_act, 1)
        with act.Fori(0, E0 // 2) as j:
            for s in range(2):
                e = j * 2 + s
                act.wait_ge(s_mine, e * 2 + 2)
                act.wait_ge(s_logit, e + 1)
                act.activation(wexp[s][:], p_l[:, 0:TILES], ACT.Exp, bias=mine[s][:, 1:2]).then_inc(s_wexp, 1)
                act.wait_ge(s_w[s], j * 64 + 64)
                for half in range(2):
                    for f in range(FT):
                        g = half * FT + f
                        act.wait_ge(s_hid_mm, e * 2 * FT + (g + 1))
                        act.activation(hid[:, f, half * 512:half * 512 + 512], p_h[f % 2][:], ACT.Gelu,
                                       bias=b1[s][:, f:f + 1]).then_inc(s_hid, 1)

    def tensor(pe):
        pe.wait_ge(s_dve, progs["n_rowmax"])
        pe.matmul(p_small[0:1, 0:P], small[:, 0:1], ident[:], start=True, stop=True).then_inc(s_pe, 1)
        pe.wait_ge(s_dve, progs["n_row"])
        pe.matmul(p_small[:, 128:129], row[:], ones[0:1, 0:1], start=True, stop=True).then_inc(s_pe, 1)
        pe.wait_ge(s_dve, progs["n_count0"])
        pe.matmul(p_small[:, 129:130], group[:], small[:, 3:4], start=True, stop=True).then_inc(s_pe, 1)
        with pe.Fori(0, 31) as r:
            pe.wait_ge(s_dve, r * 8 + (progs["n_search"] + 3))
            pe.matmul(p_small[:, 129:130], group[:], small[:, 3:4], start=True, stop=True).then_inc(s_pe, 1)
        pe.wait_ge(s_dve, progs["n_eq"])
        pe.matmul(p_small[:, 129:130], group[:], small[:, 3:4], start=True, stop=True).then_inc(s_pe, 1)
        pe.matmul(p_small[:, 130:131], before[:], small[:, 4:5], start=True, stop=True).then_inc(s_pe, 1)
        pe.wait_ge(s_dve, progs["n_sel"])
        pe.matmul(p_small[:, 131:132], before[:], small[:, 5:6], start=True, stop=True).then_inc(s_pe, 1)
        pe.wait_ge(s_act, 1)
        pe.matmul(p_small[:, 132:133], group[:], small[:, 2:3], start=True, stop=True).then_inc(s_pe, 1)
        pe.wait_ge(s_dve, progs["n_wide"])
        for i in range(TILES):
            pe.matmul(p_small[:, 192 + i * E0:192 + (i + 1) * E0], listf[:, i * P:(i + 1) * P], member[:],
                      start=True, stop=True)
        for j in range(2):
            mm = pe.matmul(p_small[:, 256 + j * E0:256 + (j + 1) * E0], wide_col[:, j, :], first[:],
                           start=True, stop=True)
        mm.then_inc(s_pe, 1)
        with pe.Fori(0, E0 // 2) as j:
            for s in range(2):
                e = j * 2 + s
                pe.wait_ge(s_gather[s], j * (16 * TILES) + 16 * TILES)
                for half in range(2):
                    for i in range(4):
                        mm = pe.transpose(p_tr[half][:, i * P:(i + 1) * P], xg[s][half * 4 + i][:], ident[:])
                    mm.then_inc(s_tr, 1)
                pe.wait_ge(s_xt, e * 2 + 2)
                pe.wait_ge(s_mine, e * 2 + 2)
                for i in range(TILES):
                    mm = pe.matmul(p_l[:, i:i + 1], xt[s][:, i * P:(i + 1) * P], mine[s][:, 0:1], start=True, stop=True)
                mm.then_inc(s_logit, 1)
                pe.wait_ge(s_w[s], j * 64 + 64)
                for half in range(2):
                    for f in range(FT):
                        g = half * FT + f
                        pe.wait_ge(s_hid, e * 2 * FT + (g + 1))
                        pe.matmul(p_h[f % 2][:], w1[s][:, f * P:(f + 1) * P], xt[s][:, half * 512:half * 512 + 512],
                                  start=True, stop=True).then_inc(s_hid_mm, 1)
                pe.wait_ge(s_hid, e * 2 * FT + (2 * FT + 2))
                for i in range(TILES):
                    pe.wait_ge(s_og, e * TILES + (i + 1))
                    pe.matmul(p_o[i % 2][:, 0:D], ones[0:1, 0:P], b2[s][:], start=True, stop=False)
                    for f in range(FT):
                        mm = pe.matmul(p_o[i % 2][:, 0:D], hid[:, f, i * P:(i + 1) * P], w2[s][:, f, :],
                                       start=False, stop=(f == FT - 1))
                    mm.then_inc(s_out_mm, 1)

    def gpsimd(pool):
        def gather(e, s):
            pool.wait_ge(s_mine, e * 2 + 2)
            for i in range(TILES):
                pool.indirect_dma_start(xg[s][i][:], None, n_rows[:, :],
                                        bass.IndirectOffsetOnAxis(ap=idx[s][:, i:i + 1], axis=0)
                                        ).then_inc(s_gather[s], 16)
        def scatter(e, s):
            need(pool, s_scatter, e * 16 * TILES)
            for i in range(TILES):
                pool.wait_ge(s_og, e * TILES + (i + 3))
                pool.indirect_dma_start(h_rows[:, :], bass.IndirectOffsetOnAxis(ap=idx[s][:, i:i + 1], axis=0),
                                        og[s][i][:], None, compute_op=ALU.add).then_inc(s_scatter, 16)

        gather(0, 0)
        for e in range(E0):
            if e + 1 < E0:
                gather(e + 1, (e + 1) % 2)
            scatter(e, e % 2)

    progs.update(b_sync=sync, b_scalar=scalar, b_vector=vector, b_gpsimd=gpsimd, b_tensor=tensor)
    return lambda eng: eng.wait_ge(s_scatter, 16 * TILES * E0)


GT = 4
GW = GT * P
NG = BATCH * RPI // GW
NH, DH = 8, 16
WIN = 64
E1, EG = 8, 4
HF = 256
NGATE = 2 + E1


def phase_c_turns(engine):
    yield None, 1, 0, 0, 1
    yield 0, 0, 1, 1, 1
    yield 1, 1, 2, 1, 2
    with engine.Fori(0, (NG - 3) // 2) as j:
        yield j * 2 + 2, 0, j * 2 + 3, j + 2, j + 2
        yield j * 2 + 3, 1, j * 2 + 4, j + 2, j + 3
    yield NG - 1, 0, None, (NG + 1) // 2, 0


def phase_c(nc, ctx, mem, a, h_rows, out, after_b, progs):
    def sb(name, shape, dt=F32):
        return mem.enter_context(nc.sbuf_tensor("c_" + name, shape, dt))

    def ps(name, shape, dt=F32):
        return mem.enter_context(nc.psum_tensor("c_" + name, shape, dt))

    def sem(name):
        return ctx.enter_context(nc.semaphore("c_" + name))

    ident, mean_w = sb("ident", [P, P]), sb("mean_w", [P, P])
    w_qkv = sb("w_qkv", [P, 3 * D])
    w_proj = sb("w_proj", [P, D])
    w_up = sb("w_up", [P, 4 * HF])
    w_so = sb("w_so", [P, 2, D])
    w_ex = sb("w_ex", [P, 2, E1 * D])
    w_gate = sb("w_gate", [P, NGATE])
    gate_b = sb("gate_b", [1, NGATE])
    bias9 = sb("bias9", [E1 + 1, D])
    cols = sb("cols", [P, 3])
    eps_cols = sb("eps_cols", [P, 2])
    ones = sb("ones", [1, P])
    earlier = sb("earlier", [P, GT, EG, EG])
    later = sb("later", [P, GT, EG, EG])

    x = [sb(f"x{s}", [P, GT, D]) for s in range(2)]
    stats, mv = sb("stats", [P, GT, 6]), sb("mv", [P, GT, 2])
    marker = sb("marker", [1, 1])
    lnv, rstd = sb("lnv", [P, GT]), sb("rstd", [P, GT])
    n3 = sb("n3", [P, GT, D])
    nt = sb("nt", [P, GW])
    qkv = sb("qkv", [P, GT, 3 * D])
    prod = [sb(f"prod{i}", [P, NH * NH * DH]) for i in range(2)]
    score = sb("score", [P, GT * NH, NH])
    top = sb("top", [P, GT * NH])
    expo = sb("expo", [P, GT * NH, NH])
    denom = sb("denom", [P, GT * NH])
    prob = sb("prob", [P, GT * NH, NH])
    o = sb("o", [P, GT, D])
    ot = sb("ot", [P, 8, GT * 16])
    dealt = [sb(f"dealt{s}", [P, NH, GT * 16]) for s in range(2)]
    h3, xc, sq, lv, r12, u, fl = (sb(n, [P, GW]) for n in ("h3", "xc", "sq", "lv", "r12", "u", "fl"))
    act_half = [sb(f"act_half{i}", [P, GW]) for i in range(2)]
    hid = [sb(f"hid{i}", [P, GW]) for i in range(4)]
    gate = sb("gate", [P, GT, NGATE])
    in1, in0 = sb("in1", [P, GT, 1]), sb("in0", [P, GT, 1])
    ea, eb, esel, eexp, ep, etop = (sb(n, [P, GT, EG]) for n in ("ea", "eb", "esel", "eexp", "ep", "etop"))
    gmax, gsum, ginv, tsum, tinv = (sb(n, [P, GT]) for n in ("gmax", "gsum", "ginv", "tsum", "tinv"))
    ge, gtt, rk = (sb(n, [P, GT, EG, EG]) for n in ("ge", "gtt", "rk"))
    rank, sel, share = (sb(n, [P, GT, EG]) for n in ("rank", "sel", "share"))
    comb = sb("comb", [P, GT, E1])
    cnt = sb("cnt", [P, GT, E1 + 1])
    cntt = sb("cntt", [E1 + 1, GW])
    base = sb("base", [P, GT, D])
    acc = [sb(f"acc{i}", [P, D]) for i in range(2)]
    res = [sb(f"res{s}", [P, GT, D]) for s in range(2)]

    heads = [nc.dram_tensor(f"heads{s}", [P, 8, GT * 16], F32, kind="Internal").ap() for s in range(2)]

    p_turn, p_gate, p_qkv, p_m = (ps(n, [P, 512]) for n in ("p_turn", "p_gate", "p_qkv", "p_m"))
    p_w = [ps(f"p_w{i}", [P, 512]) for i in range(2)]
    p_e = [ps(f"p_e{i}", [P, 512]) for i in range(2)]

    s_in, s_const = sem("in"), sem("const")
    s_x, s_heads, s_dealt, s_res = ([sem(f"{n}{s}") for s in range(2)] for n in ("x", "heads", "dealt", "res"))
    s_stats, s_mv, s_lnv, s_rstd, s_n3, s_n3t, s_nt, s_qkv_mm, s_qkv = map(
        sem, ("stats", "mv", "lnv", "rstd", "n3", "n3t", "nt", "qkv_mm", "qkv"))
    s_qk, s_score, s_top, s_dif, s_exp, s_den, s_inv, s_prob, s_pv, s_o, s_o_t, s_ot = map(
        sem, ("qk", "score", "top", "dif", "exp", "den", "inv", "prob", "pv", "o", "o_t", "ot"))
    s_proj, s_h3, s_mean, s_xc, s_sq, s_var, s_lv, s_r12, s_u, s_fl = map(
        sem, ("proj", "h3", "mean", "xc", "sq", "var", "lv", "r12", "u", "fl"))
    s_up, s_silu, s_hid, s_gate_mm, s_route, s_gexp, s_cnt_t, s_cntt, s_base_mm, s_base, s_ex, s_acc = map(
        sem, ("up", "silu", "hid", "gate_mm", "route", "gexp", "cnt_t", "cntt", "base_mm", "base", "ex", "acc"))
    LOADS = 13
    R_DIF, R_CNT, R_END = 8, 24, 24

    def sync(sp):
        after_b(sp)
        for dst, name in ((ident, "ident"), (w_qkv, "w_qkv"), (w_proj, "w_proj"), (w_up, "w_up"), (w_gate, "w_gate"),
                          (gate_b, "gate_b"), (bias9, "bias9"), (cols, "cols_c"), (w_so, "w_so"), (w_ex, "w_ex"),
                          (earlier, "earlier"), (later, "later")):
            sp.dma_start(dst[:], a[name]).then_inc(s_in, 16)
        sp.dma_start(ones[:], a["ones"]).then_inc(s_in, 16)
        for b, s, g, nb, ng in phase_c_turns(sp):
            if g is not None:
                if b is not None:
                    need(sp, s_proj, g - 1)
                sp.dma_start(x[1 - s][:], h_rows[ds(g * GW + SHIFT, GW), :].rearrange("(j p) d -> p j d", p=P)
                             ).then_inc(s_x[1 - s], 16)
                sp.wait_ge(s_ot, g + 1)
                sp.dma_start(heads[1 - s], ot[:]).then_inc(s_heads[1 - s], 16)
                sp.wait_ge(s_heads[1 - s], ng * 16)
                for j in range(8):
                    sp.dma_start(dealt[1 - s][j * DH:(j + 1) * DH, :, :],
                                 heads[1 - s][:, j, :].rearrange("(h d) c -> d h c", d=DH)
                                 ).then_inc(s_dealt[1 - s], 16)
            if b is not None:
                sp.wait_ge(s_acc, b * (9 * GT) + 9 * GT)
                sp.dma_start(out[ds(b * GW, GW), :].rearrange("(j p) d -> p j d", p=P), res[s][:]
                             ).then_inc(s_res[s], 16)
        for s in range(2):
            sp.wait_ge(s_res[s], 16 * ((NG + 1 - s) // 2))

    def tensor(pe):
        pe.wait_ge(s_in, 16 * LOADS)
        pe.wait_ge(s_const, 1)

        def attention_in(g):
            pe.wait_ge(s_n3, g + 1)
            need(pe, s_ot, g)
            for j in range(GT):
                mm = pe.transpose(p_turn[:, j * P:(j + 1) * P], n3[:, j, :], ident[:])
            mm.then_inc(s_n3t, 1)

        def qkv_mm(g, tiles):
            for j in tiles:
                pe.wait_ge(s_nt, g + 1)
                need(pe, s_qkv, g * GT + j)
                pe.matmul(p_qkv[:, 0:3 * D], nt[:, j * P:(j + 1) * P], w_qkv[:], start=True, stop=True
                          ).then_inc(s_qkv_mm, 1)

        for b, s, g, nb, ng in phase_c_turns(pe):
            if g is not None:
                attention_in(g)
            if b is not None:
                pe.wait_ge(s_dealt[s], nb * (16 * NH))
                need(pe, s_lv, b)
                pe.matmul(p_m[:].rearrange("c (w h a) -> c w h a", h=NH, a=8), w_proj[:],
                          dealt[s][:].rearrange("p h (w a) -> p w h a", a=8), start=True, stop=False,
                          skip_group_check=True)
                for j in range(GT):
                    mm = pe.matmul(p_m[:, j * P:(j + 1) * P], x[s][:, j, :], ident[:], start=False, stop=(j == GT - 1),
                                   skip_group_check=True)
                mm.then_inc(s_proj, 1)
            if g is not None:
                qkv_mm(g, (0, 1))
            if b is not None:
                pe.wait_ge(s_h3, b + 1)
                pe.matmul(p_m[:], mean_w[:], h3[:], start=True, stop=True).then_inc(s_mean, 1)
            if g is not None:
                qkv_mm(g, (2, 3))
            if b is not None:
                pe.wait_ge(s_sq, b + 1)
                pe.matmul(p_m[:], mean_w[:], sq[:], start=True, stop=True).then_inc(s_var, 1)
                pe.wait_ge(s_fl, b + 1)
                for m in range(8):
                    if m < 2:
                        need(pe, s_base, b * GT)
                    need(pe, s_hid if m % 2 else s_silu, b * 4 + m // 2)
                    pe.matmul(p_w[m % 2][:], w_up[:, m * P:(m + 1) * P], fl[:], start=True, stop=True).then_inc(s_up, 1)
                    if m == 1:
                        need(pe, s_cntt, b)
                        for j in range(GT):
                            pe.matmul(p_gate[:, j * 16:j * 16 + NGATE], fl[:, j * P:(j + 1) * P], w_gate[:],
                                      start=True, stop=False)
                            mm = pe.matmul(p_gate[:, j * 16:j * 16 + NGATE], ones[:], gate_b[:], start=False, stop=True)
                        mm.then_inc(s_gate_mm, 1)

                def experts(j):
                    for half in range(2):
                        need(pe, s_acc, b * (9 * GT) + 9 * (j - 1) + 4 * (half + 1))
                        for k in range(2):
                            mm = pe.matmul(p_e[half][:], hid[2 + k][:, j * P:(j + 1) * P],
                                           w_ex[:, k, half * 512:half * 512 + 512], start=(k == 0), stop=(k == 1))
                        mm.then_inc(s_ex, 1)

                def base_mm(j):
                    pe.wait_ge(s_base, b * GT + (j - 1)) if j >= 2 else pe.wait_ge(s_hid, b * 4 + 4)
                    w = p_w[j % 2][:, 0:D]
                    pe.matmul(w, cntt[:, j * P:(j + 1) * P], bias9[:], start=True, stop=False)
                    for k in range(2):
                        pe.matmul(w, hid[k][:, j * P:(j + 1) * P], w_so[:, k, :], start=False, stop=False)
                    pe.matmul(w, h3[:, j * P:(j + 1) * P], ident[:], start=False, stop=True).then_inc(s_base_mm, 1)

                pe.wait_ge(s_hid, b * 4 + 4)
                experts(0)
                pe.wait_ge(s_route, b * R_END + R_CNT)
                for j in range(GT):
                    mm = pe.transpose(p_gate[0:E1 + 1, j * P:(j + 1) * P], cnt[:, j, :], ident[:])
                mm.then_inc(s_cnt_t, 1)
                pe.wait_ge(s_cntt, b + 1)
                base_mm(0)
                base_mm(1)
                experts(1)
                base_mm(2)
                base_mm(3)
                experts(2)
                experts(3)
            if g is not None:
                pe.wait_ge(s_o, g * GT + GT)
                for j in range(GT):
                    mm = pe.transpose(p_turn[:, j * P:(j + 1) * P], o[:, j, :], ident[:])
                mm.then_inc(s_o_t, 1)

    def scalar(act):
        act.wait_ge(s_in, 16 * LOADS)
        act.wait_ge(s_const, 1)
        act.preload_act_table_set("natural_log_exp_and_others")
        for b, s, g, nb, ng in phase_c_turns(act):
            if g is not None:
                act.wait_ge(s_mv, g + 1)
                act.activation(lnv[:], mv[:, :, 1], ACT.Ln, bias=eps_cols[:, 0:1]).then_inc(s_lnv, 1)
                act.wait_ge(s_lnv, g + 1)
                act.activation(rstd[:], lnv[:], ACT.Exp, scale=-0.5).then_inc(s_rstd, 1)
                act.wait_ge(s_n3t, g + 1)
                act.copy(nt[:], p_turn[:]).then_inc(s_nt, 1)
            if b is not None:
                act.wait_ge(s_proj, b + 1)
                act.activation(h3[:], p_m[:], ACT.Identity, bias=cols[:, 0:1]).then_inc(s_h3, 1)

            def qkv_copy(tiles):
                for j in tiles:
                    act.wait_ge(s_qkv_mm, g * GT + (j + 1))
                    need(act, s_pv, g * GT)
                    act.copy(qkv[:, j, :], p_qkv[:, 0:3 * D]).then_inc(s_qkv, 1)
            if g is not None:
                qkv_copy((0, 1))
            if b is not None:
                act.wait_ge(s_xc, b + 1)
                act.activation(sq[:], xc[:], ACT.Square).then_inc(s_sq, 1)
            if g is not None:
                qkv_copy((2, 3))
            if b is not None:
                act.wait_ge(s_var, b + 1)
                act.activation(lv[:], p_m[:], ACT.Ln, bias=eps_cols[:, 1:2]).then_inc(s_lv, 1)
                act.wait_ge(s_lv, b + 1)
                act.activation(r12[:], lv[:], ACT.Exp, scale=-0.5).then_inc(s_r12, 1)
                act.wait_ge(s_u, b + 1)
                act.activation(fl[:], u[:], ACT.Identity, scale=cols[:, 1:2], bias=cols[:, 2:3]).then_inc(s_fl, 1)
                for i in range(4):
                    act.wait_ge(s_up, b * 8 + (2 * i + 1))
                    need(act, s_hid, b * 4 + (i - 1))
                    act.activation(act_half[i % 2][:], p_w[0][:], ACT.Silu).then_inc(s_silu, 1)
                act.preload_act_table_set("natural_log_exp_and_others")
            if g is not None:
                act.wait_ge(s_dif, g + 1)
                act.activation(expo[:], score[:], ACT.Exp, scale=DH ** -0.5).then_inc(s_exp, 1)
            if b is not None:
                act.wait_ge(s_route, b * R_END + R_DIF)
                act.activation(eexp[:], esel[:], ACT.Exp).then_inc(s_gexp, 1)
                act.wait_ge(s_cnt_t, b + 1)
                act.copy(cntt[:], p_gate[0:E1 + 1, :]).then_inc(s_cntt, 1)
                for j in range(GT):
                    act.wait_ge(s_base_mm, b * GT + (j + 1))
                    act.copy(base[:, j, :], p_w[j % 2][:, 0:D]).then_inc(s_base, 1)
            if g is not None:
                act.wait_ge(s_o_t, g + 1)
                if b is not None:
                    act.wait_ge(s_heads[s], nb * 16)
                act.copy(ot[:].rearrange("p j c -> p c j"), p_turn[:].rearrange("p (c j) -> p c j", j=8)
                         ).then_inc(s_ot, 1)

    def vector(dve):
        dve.memset(mean_w[:], 1.0 / D)
        dve.memset(eps_cols[:, 0:1], EPS)
        dve.memset(cnt[:, :, E1:E1 + 1], 1.0)
        dve.memset(eps_cols[:, 1:2], EPS * EPS / (1 + EPS)).then_inc(s_const, 1)
        dve.wait_ge(s_in, 16 * LOADS)
        for b, s, g, nb, ng in phase_c_turns(dve):
            if g is not None:
                dve.wait_ge(s_x[1 - s], ng * 16)
                for j in range(GT):
                    i = dve.bn_stats(stats[:, j, :], x[1 - s][:, j, :])
                i.then_inc(s_stats, 1)
                dve.wait_ge(s_stats, g + 1)
                dve.memset(marker[:], 0.0)
                for j in range(GT):
                    i = dve.bn_aggr(mv[:, j, :], stats[:, j, :])
                i.then_inc(s_mv, 1)
                dve.wait_ge(s_rstd, g + 1)
                dve.wait_ge(s_mv, g + 1)
                for j in range(GT):
                    i = dve.tensor_scalar(n3[:, j, :], x[1 - s][:, j, :], mv[:, j, 0:1], rstd[:, j:j + 1], ALU.subtract,
                                          ALU.mult)
                i.then_inc(s_n3, 1)

            def sum_scores(tiles):
                for j in tiles:
                    dve.wait_ge(s_qk, g * GT + (j + 1))
                    dve.tensor_reduce(score[:, j * NH:(j + 1) * NH, :],
                                      prod[j % 2][:].rearrange("p (h g d) -> p h g d", h=NH, g=NH), AX.X, ALU.add
                                      ).then_inc(s_score, 1)
            if b is not None:
                dve.wait_ge(s_mean, b + 1)
                dve.tensor_tensor(xc[:], h3[:], p_m[:], ALU.subtract).then_inc(s_xc, 1)
            if g is not None:
                sum_scores((0, 1))
            if b is not None:
                dve.wait_ge(s_r12, b + 1)
                dve.wait_ge(s_xc, b + 1)
                dve.scalar_tensor_tensor(out=u[:], in0=xc[:], scalar=(1 + EPS) ** -0.5, in1=r12[:], op0=ALU.mult,
                                         op1=ALU.mult).then_inc(s_u, 1)
            if g is not None:
                sum_scores((2, 3))
            if b is not None:
                for i in range(4):
                    dve.wait_ge(s_silu, b * 4 + (i + 1))
                    dve.wait_ge(s_up, b * 8 + (2 * i + 2))
                    dve.tensor_tensor(hid[i][:], act_half[i % 2][:], p_w[1][:], ALU.mult).then_inc(s_hid, 1)
                    if i == 0 and g is not None:
                        dve.wait_ge(s_score, g * GT + GT)
                        dve.tensor_reduce(top[:], score[:], AX.X, ALU.max).then_inc(s_top, 1)
                        dve.wait_ge(s_top, g + 1)
                        dve.tensor_tensor(score[:], score[:], top[:].unsqueeze(2).to_broadcast([P, GT * NH, NH]),
                                          ALU.subtract).then_inc(s_dif, 1)
            elif g is not None:
                dve.wait_ge(s_score, g * GT + GT)
                dve.tensor_reduce(top[:], score[:], AX.X, ALU.max).then_inc(s_top, 1)
                dve.wait_ge(s_top, g + 1)
                dve.tensor_tensor(score[:], score[:], top[:].unsqueeze(2).to_broadcast([P, GT * NH, NH]),
                                  ALU.subtract).then_inc(s_dif, 1)
            if g is not None:
                dve.wait_ge(s_exp, g + 1)
                dve.tensor_reduce(denom[:], expo[:], AX.X, ALU.add).then_inc(s_den, 1)
                dve.wait_ge(s_den, g + 1)
                dve.reciprocal(denom[:], denom[:]).then_inc(s_inv, 1)
                dve.wait_ge(s_inv, g + 1)
                dve.tensor_tensor(prob[:], expo[:], denom[:].unsqueeze(2).to_broadcast([P, GT * NH, NH]), ALU.mult
                                  ).then_inc(s_prob, 1)
            if b is not None:
                n = [0]

                def do(i):
                    n[0] += 1
                    i.then_inc(s_route, 1)
                    dve.wait_ge(s_route, b * R_END + n[0])

                wide = [P, GT, EG]
                square = [P, GT, EG, EG]
                dve.wait_ge(s_gate_mm, b + 1)
                do(dve.tensor_copy(gate[:], p_gate[:, 0:GT * 16].rearrange("p (j k) -> p j k", k=16)[:, :, 0:NGATE]))
                do(dve.tensor_tensor(in1[:], gate[:, :, 1:2], gate[:, :, 0:1], ALU.is_gt))
                do(dve.tensor_scalar(in0[:], in1[:], -1.0, 1.0, ALU.mult, ALU.add))
                do(dve.tensor_tensor(ea[:], gate[:, :, 2:2 + EG], in0[:].to_broadcast(wide), ALU.mult))
                do(dve.tensor_tensor(eb[:], gate[:, :, 2 + EG:2 + 2 * EG], in1[:].to_broadcast(wide), ALU.mult))
                do(dve.tensor_tensor(ea[:], ea[:], eb[:], ALU.add))
                do(dve.tensor_reduce(gmax[:], ea[:], AX.X, ALU.max))
                do(dve.tensor_tensor(esel[:], ea[:], gmax[:].unsqueeze(2).to_broadcast(wide), ALU.subtract))
                dve.wait_ge(s_gexp, b + 1)
                do(dve.tensor_reduce(gsum[:], eexp[:], AX.X, ALU.add))
                do(dve.reciprocal(ginv[:], gsum[:]))
                do(dve.tensor_tensor(ep[:], eexp[:], ginv[:].unsqueeze(2).to_broadcast(wide), ALU.mult))
                other = ep[:].unsqueeze(2).to_broadcast(square)
                own = ep[:].unsqueeze(3).to_broadcast(square)
                do(dve.tensor_tensor(ge[:], other, own, ALU.is_ge))
                do(dve.tensor_tensor(gtt[:], other, own, ALU.is_gt))
                do(dve.tensor_tensor(ge[:], ge[:], earlier[:], ALU.mult))
                do(dve.tensor_tensor(gtt[:], gtt[:], later[:], ALU.mult))
                do(dve.tensor_tensor(rk[:], ge[:], gtt[:], ALU.add))
                do(dve.tensor_reduce(rank[:], rk[:], AX.X, ALU.add))
                do(dve.tensor_scalar(sel[:], rank[:], 2.0, None, ALU.is_lt))
                do(dve.tensor_tensor(etop[:], ep[:], sel[:], ALU.mult))
                do(dve.tensor_reduce(tsum[:], etop[:], AX.X, ALU.add))
                do(dve.tensor_scalar(tsum[:], tsum[:], 1e-8, None, ALU.add))
                do(dve.reciprocal(tinv[:], tsum[:]))
                do(dve.tensor_tensor(share[:], etop[:], tinv[:].unsqueeze(2).to_broadcast(wide), ALU.mult))
                dve.tensor_tensor(cnt[:, :, 0:EG], sel[:], in0[:].to_broadcast(wide), ALU.mult)
                dve.tensor_tensor(cnt[:, :, EG:E1], sel[:], in1[:].to_broadcast(wide), ALU.mult)
                dve.tensor_tensor(comb[:, :, 0:EG], share[:], in0[:].to_broadcast(wide), ALU.mult)
                do(dve.tensor_tensor(comb[:, :, EG:E1], share[:], in1[:].to_broadcast(wide), ALU.mult))
                assert n[0] == R_END

                def add_experts(j):
                    c0 = b * (9 * GT) + 9 * j
                    for e in range(E1):
                        if e % EG == 0:
                            dve.wait_ge(s_ex, b * (2 * GT) + (2 * j + e // EG + 1))
                        y = p_e[e // EG][:, e % EG * D:(e % EG + 1) * D]
                        w = comb[:, j, e:e + 1]
                        if e == 1:
                            dve.tensor_scalar(acc[1][:], y, w, None, ALU.mult).then_inc(s_acc, 1)
                            continue
                        if e == 0:
                            dve.wait_ge(s_base, b * GT + (j + 1))
                        else:
                            dve.wait_ge(s_acc, c0 + (e - 1))
                        dve.scalar_tensor_tensor(out=acc[e % 2][:], in0=y, scalar=w,
                                                 in1=base[:, j, :] if e == 0 else acc[e % 2][:], op0=ALU.mult,
                                                 op1=ALU.add).then_inc(s_acc, 1)
                    dve.wait_ge(s_acc, c0 + 8)
                    dve.tensor_tensor(res[s][:, j, :], acc[0][:], acc[1][:], ALU.add).then_inc(s_acc, 1)
                    dve.wait_ge(s_acc, c0 + 9)

                need(dve, s_res[s], nb * 16 - 16)
            for j in range(GT):
                if b is not None:
                    add_experts(j)
                if g is not None:
                    dve.wait_ge(s_pv, g * GT + (j + 1))
                    dve.tensor_reduce(o[:, j, :], prod[j % 2][:].rearrange("p (h g) -> p h g", g=NH), AX.X, ALU.add
                                      ).then_inc(s_o, 1)

    def gpsimd(pool):
        for b, s, g, nb, ng in phase_c_turns(pool):
            if g is None:
                continue
            for j in range(GT):
                pool.wait_ge(s_qkv, g * GT + (j + 1))
                if j >= 2:
                    pool.wait_ge(s_score, g * GT + (j - 1))
                else:
                    need(pool, s_o, g * GT + (j - 1))
                q, k = qkv[:, j, 0:D], qkv[:, j, D:2 * D]
                pool.tensor_tensor(prod[j % 2][:].rearrange("p (h g d) -> p h g d", h=NH, g=NH),
                                   q.rearrange("p (h d) -> p h d", d=DH).unsqueeze(2).to_broadcast([P, NH, NH, DH]),
                                   k.rearrange("p (g d) -> p g d", d=DH).unsqueeze(1).to_broadcast([P, NH, NH, DH]),
                                   ALU.mult).then_inc(s_qk, 1)
            for j in range(GT):
                pool.wait_ge(s_prob, g + 1)
                if j >= 2:
                    pool.wait_ge(s_o, g * GT + (j - 1))
                v = qkv[:, j, 2 * D:3 * D]
                pool.tensor_tensor(prod[j % 2][:].rearrange("p (h d g) -> p h d g", h=NH, g=NH),
                                   prob[:, j * NH:(j + 1) * NH, :].unsqueeze(2).to_broadcast([P, NH, DH, NH]),
                                   v.rearrange("p (g d) -> p d g", d=DH).unsqueeze(1).to_broadcast([P, NH, DH, NH]),
                                   ALU.mult).then_inc(s_pv, 1)

    progs.update(c_sync=sync, c_scalar=scalar, c_vector=vector, c_gpsimd=gpsimd, c_tensor=tensor)


def lay_out(i):
    f = {k: np.asarray(v) for k, v in i.items()}
    x = f["x"].reshape(BATCH, 3, 56, 4, 56, 4).transpose(1, 3, 5, 0, 2, 4).reshape(PV, BATCH * NPATCH)
    halves = lambda v: v.reshape(2, P, -1).transpose(1, 0, 2)
    wbc = np.concatenate([f["L0_attn_W_B"], f["L0_attn_W_C"]], 0)
    z = np.zeros_like(wbc)
    wbc = halves(np.concatenate([wbc, z, wbc, wbc], 0).T)
    cols = np.concatenate([
        f["L0_tok_b"][:, None], f["cls_tok"].reshape(D, 1), f["L0_tok_cls"].reshape(D, 1),
        f["L0_attn_ln_g"][:, None], f["L0_attn_ln_b"][:, None], f["L0_attn_conv_b"].reshape(2, P).T,
        f["L0_attn_b_dt"].reshape(2, P).T, halves(f["L0_attn_conv_w"].reshape(DI, KC)).reshape(P, 2 * KC),
        halves(f["L0_attn_log_A"]).reshape(P, 2 * NS)], 1)
    picks = np.zeros((P, 2 * NS), np.float32)
    for first in (0, 64, 96):
        picks[first:first + 2 * NS] = np.eye(2 * NS)
    m = {"patches": x, "wtok": f["L0_tok_W"].T, "cols": cols, "w_in": f["L0_attn_W_in"].T,
         "ident": np.eye(P, dtype=np.float32), "picks": picks, "w_bc": wbc, "w_dt": halves(f["L0_attn_W_dt"].T),
         "w_out": halves(f["L0_attn_W_out"].T), "w_r": f["L0_ffn_Wr"]}
    part, col = np.arange(P)[:, None], np.arange(SPAN)[None, :]
    token = np.minimum(part % 16 * SPAN + col, NTOK - 1)
    image, t = token // T, token % T
    m["rows"] = (image * RB + np.where(t < SHIFT, t + T, t)).astype(np.int32)
    m["iota"] = np.broadcast_to(CAP + 1 + col, (P, SPAN)).astype(np.float32)
    q = np.arange(P)
    same = q[:, None] // 16 == q[None, :] // 16
    m["group"] = same.astype(np.float32)
    m["before"] = (same & (q[:, None] < q[None, :])).astype(np.float32)
    m["member"] = (q[:, None] // 16 == np.arange(E0)[None, :]).astype(np.float32)
    m["first"] = (q[:, None] == 16 * np.arange(E0)[None, :]).astype(np.float32)
    m["w1"] = f["L0_ffn_W1"].reshape(E0 * D, FF)
    m["w2"] = f["L0_ffn_W2"].reshape(E0, FF // P, P, D).transpose(0, 2, 1, 3).reshape(E0 * P, FF)
    m["b1"] = f["L0_ffn_b1"].reshape(E0, FF // P, P).transpose(0, 2, 1).reshape(E0 * P, FF // P)
    m["b2"] = f["L0_ffn_b2"]
    m["w_qkv"] = f["L1_attn_w_qkv"].T
    m["w_proj"] = f["L1_attn_w_proj"].T
    pairs = lambda v: v.reshape(2, 2, P, D).transpose(1, 0, 2, 3).reshape(4 * P, D)
    m["w_up"] = np.concatenate([pairs(f["L1_ffn_shared_in_w"]), pairs(f["L1_ffn_expert_in_w"])], 0).T
    m["w_so"] = halves(f["L1_ffn_shared_out_w"].T)
    m["w_ex"] = halves(f["L1_ffn_expert_out_weight"].transpose(2, 0, 1).reshape(HF, E1 * D))
    m["w_gate"] = np.concatenate([f["L1_ffn_group_gate_w"], f["L1_ffn_expert_gate_w"]], 0).T
    m["gate_b"] = np.concatenate([f["L1_ffn_group_bias"], f["L1_ffn_expert_bias"]])[None]
    m["bias9"] = np.concatenate([f["L1_ffn_expert_out_bias"], f["L1_ffn_shared_out_b"][None]], 0)
    m["cols_c"] = np.stack([f["L1_attn_b_proj"], f["L1_ffn_ln_scale"], f["L1_ffn_ln_bias"]], 1)
    e = np.arange(EG)
    m["earlier"] = np.broadcast_to(e[None, :] < e[:, None], (P, GT, EG, EG)).astype(np.float32)
    m["later"] = np.broadcast_to(e[None, :] > e[:, None], (P, GT, EG, EG)).astype(np.float32)
    m["ones"] = np.ones((1, P), np.float32)
    return {k: np.ascontiguousarray(v) for k, v in m.items()}


def kernel(**inputs):
    import concourse.bacc as bacc
    from concourse.bass_utils import run_bass_kernel_spmd

    nc = bacc.Bacc("TRN2", target_bir_lowering=False, num_devices=1)
    arrays = lay_out(inputs)
    args = {k: nc.dram_tensor(f"in_{k}", v.shape, mybir.dt.from_np(v.dtype), kind="ExternalInput").ap()
            for k, v in arrays.items()}
    rolled = nc.dram_tensor("rolled", (BATCH * RPI, D), F32, kind="ExternalOutput").ap()
    build(nc, args, rolled)
    r = run_bass_kernel_spmd(nc, [{f"in_{k}": v for k, v in arrays.items()}], core_ids=[0])
    got = r.results[0]["rolled"].reshape(BATCH, RPI, D)[:, :T]
    return np.concatenate([got[:, T - SHIFT:], got[:, :T - SHIFT]], 1)
```

```python
from contextlib import ExitStack

import numpy as np

import concourse.bass as bass
from concourse import mybir
from concourse.alu_op_type import AluOpType as ALU

F32 = mybir.dt.float32
BF16 = mybir.dt.bfloat16
I32 = mybir.dt.int32
U32 = mybir.dt.uint32
ACT = mybir.ActivationFunctionType
AX = mybir.AxisListType
ds = bass.ds

P = 128
BATCH = 4
D = 128
DI = 256
NS = 16
KC = 4
PV = 48
NPATCH = 3136
T = NPATCH + 2
NTOK = BATCH * T
W = 448
NCH = NPATCH // W
TT = 112
NT = W // TT
SHIFT = 32
RPI = 3200
RB = RPI
ROWS = BATCH * RB + SHIFT
EPS = 1e-5
E0 = 8
CAP = 1024
FF = 512
SPAN = 785
NLG = 16 * SPAN
STEPS = 2 * NS
H_RING, DA_RING, DBX_RING, HC_RING, CS_RING = 16, 4, 3, 8, 4
SUM_LAG = 6

PRE_USES = (("tok", "xm1", "z0", "dt0"), ("mean", "var", "xm0", "z1", "bc", "dt1"))
POST_USES = (("out", "mean2", "logit", "trh"), ("var2", "trn"))
ORDER = ("tok", "mean", "out", "var", "mean2", "xm0", "xm1", "var2", "z0", "z1", "logit", "bc", "dt0", "dt1",
         "trh", "trn")


def need(eng, sem, value):
    if isinstance(value, int) and value <= 0:
        return
    eng.wait_ge(sem, value)


class Turn:

    def __init__(self, q, slot, w=W, scan=True, pre=True, post=True, post_w=W, pre_w=W, pre_at=None, post_at=None,
                 fresh=False, reset=False):
        self.first = isinstance(q, int) and q == 0
        self.q, self.slot, self.w, self.scan, self.pre, self.post = q, slot, w, scan, pre, post
        self.pre_w, self.post_w = pre_w, post_w
        self.pre_at, self.post_at = pre_at, post_at
        self.fresh = fresh
        self.reset = reset

    def bank_of(self, use):
        return 0 if use in PRE_USES[0] + POST_USES[0] else 1

    def nth(self, use):
        b = self.bank_of(use)
        mine = [u for u in ORDER if u in (PRE_USES[b] if self.pre else ()) + (POST_USES[b] if self.post else ())
                and not (u == "tok" and self.pre_w != W)]
        before = (len(PRE_USES[b]) - (b == 0)) * (self.has(0)) + len(PRE_USES[b]) * (self.has(1))
        if self.has(2):
            before = before + (self.q - 1) * (len(PRE_USES[b]) + len(POST_USES[b]))
        if isinstance(self.q, int) and self.q == 29:
            before -= len(PRE_USES[b])
        return before + mine.index(use)

    def has(self, n):
        return (not isinstance(self.q, int)) or self.q + 1 > n


def phase_a_turns(engine):
    yield Turn(-1, 0, scan=False, post=False, pre_w=2)
    yield Turn(0, 1, w=2, post=False, pre_at=(0, 0), fresh=True)
    for pair in range(BATCH // 2):
        q0 = 2 * NCH * pair
        last = pair == BATCH // 2 - 1
        yield Turn(q0 + 1, 0, pre_at=(2 * pair + 1, 0), post_w=2 if pair == 0 else W,
                   post_at=(2 * pair - 1, NCH - 1))
        with engine.Fori(0, NCH - 1) as c:
            yield Turn(q0 + 2 + c * 2, 1, pre_at=(2 * pair, c + 1), post_at=(2 * pair, c))
            yield Turn(q0 + 3 + c * 2, 0, pre_at=(2 * pair + 1, c + 1), post_at=(2 * pair + 1, c))
        yield Turn(q0 + 2 * NCH, 1, pre=not last, pre_at=(2 * pair + 2, 0), post_at=(2 * pair, NCH - 1),
                   fresh=not last, reset=not last)
    yield Turn(2 * NCH * (BATCH // 2) + 1, 0, scan=False, pre=False, post_at=(BATCH - 1, NCH - 1))


def build(nc, a, out, upto="C", debug=None):
    debug = debug or {}
    with ExitStack() as ctx:
        def sb(name, shape, dt=F32):
            return ctx.enter_context(nc.sbuf_tensor(name, shape, dt))

        def ps(name, shape, dt=F32):
            return ctx.enter_context(nc.psum_tensor(name, shape, dt))

        def sem(name):
            return ctx.enter_context(nc.semaphore(name))

        def dram(name, shape, dt=F32):
            return debug[name] if name in debug else nc.dram_tensor(name, shape, dt, kind="Internal").ap()

        h_rows = dram("h_rows", [ROWS, D])
        n_rows = dram("n_rows", [ROWS, D])
        logits = dram("logits", [E0, NLG])
        block = ctx.enter_context(nc.Block())
        progs = {}
        with ExitStack() as mem:
            phase_a(nc, ctx, mem, a, h_rows, n_rows, logits, progs)
        if upto >= "B":
            with ExitStack() as mem:
                progs["after_b"] = phase_b(nc, ctx, mem, a, h_rows, n_rows, logits, progs["after_a"], progs)
        if upto >= "C":
            with ExitStack() as mem:
                phase_c(nc, ctx, mem, a, h_rows, out, progs["after_b"], progs)
        if upto == "B":
            progs["z_sync"] = progs["after_b"]
        if upto == "A":
            progs["z_sync"] = progs["after_a"]

        @block.sync
        def _(sp):
            progs["a_sync"](sp)
            for part in ("b", "c", "z"):
                if part + "_sync" in progs:
                    progs[part + "_sync"](sp)

        @block.vector
        def _(dve):
            progs["a_vector"](dve)
            for part in ("b", "c", "z"):
                if part + "_vector" in progs:
                    progs[part + "_vector"](dve)

        @block.scalar
        def _(act):
            progs["a_scalar"](act)
            for part in ("b", "c", "z"):
                if part + "_scalar" in progs:
                    progs[part + "_scalar"](act)

        @block.gpsimd
        def _(pool):
            progs["a_gpsimd"](pool)
            for part in ("b", "c", "z"):
                if part + "_gpsimd" in progs:
                    progs[part + "_gpsimd"](pool)

        @block.tensor
        def _(pe):
            progs["a_tensor"](pe)
            for part in ("b", "c", "z"):
                if part + "_tensor" in progs:
                    progs[part + "_tensor"](pe)


def phase_a(nc, ctx, mem, a, h_rows, n_rows, logits, progs):
    def sb(name, shape, dt=F32):
        return mem.enter_context(nc.sbuf_tensor("a_" + name, shape, dt))

    def ps(name, shape, dt=F32):
        return mem.enter_context(nc.psum_tensor("a_" + name, shape, dt))

    def sem(name):
        return ctx.enter_context(nc.semaphore("a_" + name))

    wtok = sb("wtok", [PV, D])
    w_in = sb("w_in", [P, 2 * DI])
    w_bc = sb("w_bc", [P, 2, P])
    w_dt = sb("w_dt", [P, 2, DI])
    w_out = sb("w_out", [P, 2, D])
    w_r = sb("w_r", [P, E0])
    cols = sb("cols", [P, 49])
    btok, cls2, gain, bias = cols[:, 0:1], cols[:, 1:3], cols[:, 3:4], cols[:, 4:5]
    conv_b, dt_b, taps, log_a = cols[:, 5:7], cols[:, 7:9], cols[:, 9:17], cols[:, 17:49]
    neg_a = sb("neg_a", [P, 2 * NS])
    ident = sb("ident", [P, P])
    mean_w = sb("mean_w", [P, P])
    zero_rows = sb("zero_rows", [RB - T, D])
    least = sb("least", [E0, NLG - NTOK])
    eps_cols = sb("eps_cols", [P, 2])
    picks = sb("picks", [P, 2 * NS])
    sel = sb("sel", [P, 2 * NS, P], BF16)

    xp = [sb(f"xp{s}", [PV, W]) for s in range(2)]
    h0 = sb("h0", [P, W])
    xc = sb("xc", [P, W])
    sq = sb("sq", [P, W])
    r1 = sb("r1", [P, W])
    r12 = sb("r12", [P, W])
    l1, l12, l2 = sb("l1", [P, W]), sb("l12", [P, W]), sb("l2", [P, W])
    u = sb("u", [P, W])
    n1 = sb("n1", [P, W])
    xn = sb("xn", [P, W])
    xr = [sb(f"xr{s}", [P, 2, KC - 1 + W]) for s in range(2)]
    tail0 = sb("tail0", [P, 2, KC - 1])
    cv = sb("cv", [P, 2, W])
    xm = sb("xm", [P, 2, W])
    bcr = sb("bcr", [P, W])
    spx = sb("spx", [P, 2, W])
    spe = sb("spe", [P, 2, W])
    spl = sb("spl", [P, 2, W])
    yt = sb("yt", [P, 2, W])
    hn = [sb(f"hn{s}", [P, W]) for s in range(2)]
    sz = [sb(f"sz{s}", [P, 2, W]) for s in range(2)]
    dt = [sb(f"dt{s}", [P, 2, W]) for s in range(2)]
    dtx = [sb(f"dtx{s}", [P, 2, W]) for s in range(2)]
    bc = [sb(f"bc{s}", [P, W], BF16) for s in range(2)]
    da = sb("da", [P, DA_RING, W])
    dbx = sb("dbx", [P, 4, W])
    h = sb("h", [P, H_RING, W])
    hc = sb("hc", [P, HC_RING, W])
    cs = sb("cs", [P, CS_RING, W])
    carry = [sb(f"state{s}", [P, STEPS]) for s in range(2)]
    carry0 = sb("state_prefix", [P, STEPS])
    yz = sb("yz", [P, 2, W])
    h1 = sb("h1", [P, W])
    xc2 = sb("xc2", [P, W])
    sq2 = sb("sq2", [P, W])
    r2 = sb("r2", [P, W])
    n2 = sb("n2", [P, W])
    lg = sb("lg", [E0, W])
    th = sb("th", [TT, NT * D])
    tn = sb("tn", [TT, NT * D])

    b_bank = [ps(f"b_bank{i}", [P, 512]) for i in range(2)]
    c_bank = [ps(f"c_bank{i}", [P, 512]) for i in range(2)]
    y_bank = [ps(f"y_bank{i}", [P, 512]) for i in range(2)]
    work = [ps(f"work{i}", [P, 512]) for i in range(2)]

    s_weights = sem("weights")
    s_const, s_sel, s_neg_a = sem("const"), sem("sel"), sem("neg_a")
    s_patches = [sem(f"patches{s}") for s in range(2)]
    s_full = [sem(f"full{i}") for i in range(2)]
    s_free = [sem(f"free{i}") for i in range(2)]
    s_h0, s_sq, s_r1, s_u, s_n1, s_hn, s_xn = map(sem, ("h0", "sq", "r1", "u", "n1", "hn", "xn"))
    s_fresh = sem("fresh")
    s_l1, s_r12, s_r2 = map(sem, ("l1", "r12", "r2"))
    s_tap0, s_conv_step, s_conv, s_tail, s_xm = map(sem, ("tap0", "conv_step", "conv", "tail", "xm"))
    s_bch, s_bcm, s_bc = map(sem, ("bch", "bcm", "bc"))
    s_abs, s_spe, s_spl, s_spu, s_spd, s_spm, s_dt, s_dtx = map(
        sem, ("abs", "spe", "spl", "spu", "spd", "spm", "dt", "dtx"))
    s_b, s_c, s_cs, s_da, s_dbx, s_scan, s_carry, s_hc, s_sum = map(
        sem, ("b", "c", "cs", "da", "dbx", "scan", "carry", "hc", "sum"))
    s_reset = sem("reset")
    s_yz, s_sq2, s_n2 = map(sem, ("yz", "sq2", "n2"))
    s_again, s_end = sem("again"), sem("end")
    s_lg_out, s_th_out, s_tn_out = sem("lg_out"), sem("th_out"), sem("tn_out")
    N_WEIGHTS = 9

    def sync(sp):
        for dst, src in ((wtok[:], a["wtok"]), (cols[:], a["cols"]), (w_in[:], a["w_in"]), (ident[:], a["ident"]),
                         (picks[:], a["picks"]), (w_bc[:], a["w_bc"]), (w_dt[:], a["w_dt"]), (w_out[:], a["w_out"]),
                         (w_r[:], a["w_r"])):
            sp.dma_start(dst, src).then_inc(s_weights, 16)
        for t in phase_a_turns(sp):
            if t.pre and t.pre_w == W:
                image, c = t.pre_at
                p = t.q + 1
                if not (isinstance(t.q, int) and p <= 2):
                    need(sp, s_hn, p - 1)
                sp.dma_start(xp[t.slot ^ 1][:], a["patches"][:, ds(image * NPATCH + c * W, W)]).then_inc(s_patches[t.slot ^ 1], 16)
            if t.post and t.post_w == 2:
                for b in range(BATCH):
                    taken(sp, t, "logit")
                    sp.dma_start(logits[:, b * T:b * T + 2], lg[:, 0:2]).then_inc(s_lg_out, 16)
                for b in range(BATCH):
                    taken(sp, t, "trh")
                    sp.dma_start(h_rows[b * RB:b * RB + 2, :], th[0:2, 0:D]).then_inc(s_th_out, 16)
                for b in range(BATCH):
                    taken(sp, t, "trn")
                    sp.dma_start(n_rows[b * RB:b * RB + 2, :], tn[0:2, 0:D]).then_inc(s_tn_out, 16)
            elif t.post:
                image, c = t.post_at
                taken(sp, t, "logit")
                sp.dma_start(logits[:, ds(image * T + 2 + c * W, W)], lg[:]).then_inc(s_lg_out, 16)
                for use, tile, rows, done in (("trh", th, h_rows, s_th_out), ("trn", tn, n_rows, s_tn_out)):
                    taken(sp, t, use)
                    sp.dma_start(rows[ds(image * RB + 2 + c * W, W), :].rearrange("(j p) d -> p j d", p=TT),
                                 tile[:].rearrange("p (j d) -> p j d", j=NT)).then_inc(done, 16)
        outs = BATCH + 2 * NCH * (BATCH // 2)
        for done in (s_lg_out, s_th_out, s_tn_out):
            sp.wait_ge(done, 16 * outs)
        for b in range(BATCH):
            for rows in (h_rows, n_rows):
                sp.dma_start(rows[b * RB + T:b * RB + T + SHIFT, :], rows[b * RB:b * RB + SHIFT, :]
                             ).then_inc(s_again, 16)
        sp.wait_ge(s_again, 16 * 2 * BATCH)
        for rows in (h_rows, n_rows):
            for b in range(BATCH):
                sp.dma_start(rows[b * RB + T + SHIFT:(b + 1) * RB + SHIFT, :], zero_rows[:]).then_inc(s_end, 16)
            sp.dma_start(rows[0:SHIFT, :], zero_rows[0:SHIFT, :]).then_inc(s_end, 16)
        sp.dma_start(logits[:, NTOK:NLG], least[:]).then_inc(s_end, 16)

    def bank(t, use):
        return work[t.bank_of(use)]

    def result(eng, t, use):
        eng.wait_ge(s_full[t.bank_of(use)], t.nth(use) + 1)
        return s_free[t.bank_of(use)]

    def taken(eng, t, use):
        eng.wait_ge(s_free[t.bank_of(use)], t.nth(use) + 1)

    def h0_ready(eng, t):
        if t.pre_w == W:
            taken(eng, t, "tok")
        else:
            eng.wait_ge(s_h0, 1)

    def tensor(pe):
        def begin(t, use):
            need(pe, s_free[t.bank_of(use)], t.nth(use))
            return bank(t, use)

        def end(t, use, mm):
            mm.then_inc(s_full[t.bank_of(use)], 1)

        def spread(q, slot, n, w):
            if n == 0:
                pe.wait_ge(s_bc, q + 1)
            need(pe, s_dbx, q * STEPS + 2 * n - 2)
            pe.matmul(b_bank[n % 2][:, 0:w], sel[:, n, :], bc[slot][:, 0:w], start=True, stop=True).then_inc(s_b, 1)
            need(pe, s_cs, q * NS + n - 1)
            pe.matmul(c_bank[n % 2][:, 0:w], sel[:, NS + n, :], bc[slot][:, 0:w], start=True, stop=True).then_inc(s_c, 1)

        def add(t, k):
            n, d = divmod(k, 2)
            if n == 0:
                need(pe, s_yz, t.q * 2)
            pe.wait_ge(s_hc, t.q * STEPS + (k + 1))
            pe.matmul(y_bank[d][:, 0:t.w], ident[:], hc[:, k % HC_RING, 0:t.w], start=(n == 0), stop=(n == NS - 1)
                      ).then_inc(s_sum, 1)

        pe.wait_ge(s_weights, 16 * N_WEIGHTS)
        pe.wait_ge(s_const, 1)
        pe.wait_ge(s_sel, 1)
        for t in phase_a_turns(pe):
            p, pw = t.q + 1, t.pre_w
            rw, so = t.post_w, t.slot ^ 1
            for k in range(STEPS):
                if t.scan and k % 2 == 1:
                    n = (k - 1) // 2 + 2
                    if n < NS:
                        spread(t.q, t.slot, n, t.w)
                if t.scan and k >= SUM_LAG:
                    add(t, k - SUM_LAG)
                if t.pre:
                    if k == 1 and pw == W:
                        o = begin(t, "tok")
                        pe.wait_ge(s_patches[so], (t.pre_at[0] // 2 * NCH + 1 + t.pre_at[1]) * 16)
                        end(t, "tok", pe.matmul(o[:, 0:pw], wtok[:], xp[so][:], start=True, stop=True))
                    if k == 3:
                        o = begin(t, "mean")
                        h0_ready(pe, t)
                        end(t, "mean", pe.matmul(o[:, 0:pw], mean_w[:], h0[:, 0:pw], start=True, stop=True))
                    if k == 6:
                        o = begin(t, "var")
                        pe.wait_ge(s_sq, p + 1)
                        end(t, "var", pe.matmul(o[:, 0:pw], mean_w[:], sq[:, 0:pw], start=True, stop=True))
                    for use, at, m in (("xm0", 10, 0), ("xm1", 10, 1), ("z0", 13, 2), ("z1", 15, 3)):
                        if k == at:
                            o = begin(t, use)
                            pe.wait_ge(s_xn, p + 1)
                            end(t, use, pe.matmul(o[:, 0:pw], w_in[:, m * P:(m + 1) * P], xn[:, 0:pw], start=True,
                                                  stop=True))
                    if k == 17:
                        o = begin(t, "bc")
                        pe.wait_ge(s_xm, p + 1)
                        for j in range(2):
                            mm = pe.matmul(o[:, 0:pw], w_bc[:, j, :], xm[:, j, 0:pw], start=(j == 0), stop=(j == 1))
                        end(t, "bc", mm)
                    for use, at, m in (("dt0", 18, 0), ("dt1", 20, 1)):
                        if k == at:
                            o = begin(t, use)
                            for j in range(2):
                                mm = pe.matmul(o[:, 0:pw], w_dt[:, j, m * P:(m + 1) * P], xm[:, j, 0:pw],
                                               start=(j == 0), stop=(j == 1))
                            end(t, use, mm)
                if t.post:
                    if k == 5:
                        o = begin(t, "out")
                        pe.wait_ge(s_yz, t.q * 2)
                        pe.wait_ge(s_hn, t.q)
                        for j in range(2):
                            pe.matmul(o[:, 0:rw], w_out[:, j, :], yz[:, j, 0:rw], start=(j == 0), stop=False)
                        end(t, "out", pe.matmul(o[:, 0:rw], ident[:], hn[so][:, 0:rw], start=False, stop=True))
                    if k == 9:
                        o = begin(t, "mean2")
                        taken(pe, t, "out")
                        end(t, "mean2", pe.matmul(o[:, 0:rw], mean_w[:], h1[:, 0:rw], start=True, stop=True))
                    if k == 12:
                        o = begin(t, "var2")
                        pe.wait_ge(s_sq2, t.q)
                        end(t, "var2", pe.matmul(o[:, 0:rw], mean_w[:], sq2[:, 0:rw], start=True, stop=True))
                    if k == 16:
                        o = begin(t, "logit")
                        pe.wait_ge(s_n2, t.q)
                        end(t, "logit", pe.matmul(o[0:E0, 0:rw], w_r[:], n2[:, 0:rw], start=True, stop=True))
                    for use, at, src in (("trh", 22, h1), ("trn", 24, n2)):
                        if k == at:
                            o = begin(t, use)
                            tiles = NT if rw == W else 1
                            m = min(rw, TT)
                            for j in range(tiles):
                                mm = pe.transpose(o[0:m, j * D:(j + 1) * D], src[:, j * TT:j * TT + m], ident[:])
                            end(t, use, mm)
            if t.pre:
                for n in range(2):
                    spread(p, so, n, pw)
            if t.scan:
                for k in range(STEPS - SUM_LAG, STEPS):
                    add(t, k)

    def scalar(act):
        act.wait_ge(s_weights, 16 * N_WEIGHTS)
        act.wait_ge(s_const, 1)
        act.preload_act_table_set("natural_log_exp_and_others")
        act.activation(neg_a[:], log_a, ACT.Exp).then_inc(s_neg_a, 1)
        for t in phase_a_turns(act):
            p, pw, so = t.q + 1, t.pre_w, t.slot ^ 1
            rw = t.post_w
            for k in range(STEPS):
                if t.scan:
                    n, d = divmod(k, 2)
                    if k == 0:
                        act.wait_ge(s_dt, t.q + 1)
                        act.wait_ge(s_neg_a, 2)
                    need(act, s_scan, t.q * STEPS + (k + 1 - DA_RING))
                    act.activation(da[:, k % DA_RING, 0:t.w], dt[t.slot][:, d, 0:t.w], ACT.Exp,
                                   scale=neg_a[:, d * NS + n:d * NS + n + 1]).then_inc(s_da, 1)
                    if d == 0:
                        act.wait_ge(s_c, t.q * NS + (n + 1))
                        need(act, s_hc, t.q * STEPS + 2 * (n - CS_RING) + 2)
                        act.copy(cs[:, n % CS_RING, 0:t.w], c_bank[n % 2][:, 0:t.w]).then_inc(s_cs, 1)
                if t.pre:
                    if k == 2:
                        need(act, s_hn, p)
                        if pw == W:
                            free = result(act, t, "tok")
                            act.activation(h0[:, 0:pw], bank(t, "tok")[:, 0:pw], ACT.Identity, bias=btok
                                           ).then_inc(free, 1)
                        else:
                            act.copy(h0[:, 0:2], cls2).then_inc(s_h0, 1)
                    if k == 5:
                        taken(act, t, "mean")
                        act.activation(sq[:, 0:pw], xc[:, 0:pw], ACT.Square).then_inc(s_sq, 1)
                    if k == 7:
                        free = result(act, t, "var")
                        v = bank(t, "var")[:, 0:pw]
                        act.activation(l1[:, 0:pw], v, ACT.Ln, bias=eps_cols[:, 0:1]).then_inc(s_l1, 1)
                        act.activation(l12[:, 0:pw], v, ACT.Ln, bias=eps_cols[:, 1:2]).then_inc(free, 1)
                        act.wait_ge(s_l1, p + 1)
                        need(act, s_n1, p)
                        act.activation(r1[:, 0:pw], l1[:, 0:pw], ACT.Exp, scale=-0.5).then_inc(s_r1, 1)
                        taken(act, t, "var")
                        act.activation(r12[:, 0:pw], l12[:, 0:pw], ACT.Exp, scale=-0.5).then_inc(s_r12, 1)
                    if k == 9:
                        act.wait_ge(s_u, p + 1)
                        act.activation(xn[:, 0:pw], u[:, 0:pw], ACT.Identity, scale=gain, bias=bias).then_inc(s_xn, 1)
                    if k == 11:
                        for d, use in enumerate(("xm0", "xm1")):
                            free = result(act, t, use)
                            act.copy(xr[so][:, d, KC - 1:KC - 1 + pw], bank(t, use)[:, 0:pw]).then_inc(free, 1)
                        for d, use in enumerate(("xm0", "xm1")):
                            taken(act, t, use)
                            act.activation(cv[:, d, 0:pw], xr[so][:, d, KC - 1:KC - 1 + pw], ACT.Identity,
                                           scale=taps[:, d * KC + KC - 1:d * KC + KC], bias=conv_b[:, d:d + 1]
                                           ).then_inc(s_tap0, 1)
                    if k == 16:
                        for d, use in enumerate(("z0", "z1")):
                            free = result(act, t, use)
                            act.activation(sz[so][:, d, 0:pw], bank(t, use)[:, 0:pw], ACT.Silu).then_inc(free, 1)
                        act.wait_ge(s_conv, (p + 1) * 2)
                        need(act, s_dtx, p)
                        act.activation(xm[:, :, 0:pw], cv[:, :, 0:pw], ACT.Silu).then_inc(s_xm, 1)
                        act.preload_act_table_set("natural_log_exp_and_others")
                    if k == 18:
                        act.wait_ge(s_full[t.bank_of("bc")], t.nth("bc") + 1)
                        act.copy(bc[so][:, 0:pw], bank(t, "bc")[:, 0:pw]).then_inc(s_bch, 1)
                    if k == 20:
                        taken(act, t, "bc")
                        act.copy(bc[so][64:128, 0:pw], bcr[64:128, 0:pw]).then_inc(s_bcm, 1)
                    if k == 19 or k == 22:
                        d = int(k == 22)
                        free = result(act, t, f"dt{d}")
                        need(act, s_dt, p)
                        act.activation(spx[:, d, 0:pw], bank(t, f"dt{d}")[:, 0:pw], ACT.Identity,
                                       bias=dt_b[:, d:d + 1]).then_inc(free, 1)
                    if k == 23:
                        for d in range(2):
                            taken(act, t, f"dt{d}")
                        act.activation(spe[:, :, 0:pw], spx[:, :, 0:pw], ACT.Abs).then_inc(s_abs, 1)
                        act.wait_ge(s_abs, p + 1)
                        act.activation(spe[:, :, 0:pw], spe[:, :, 0:pw], ACT.Exp, scale=-1.0).then_inc(s_spe, 1)
                        act.wait_ge(s_spe, p + 1)
                        act.activation(spl[:, :, 0:pw], spe[:, :, 0:pw], ACT.Ln, bias=1.0).then_inc(s_spl, 1)
                if t.post:
                    if k == 8:
                        free = result(act, t, "out")
                        act.copy(h1[:, 0:rw], bank(t, "out")[:, 0:rw]).then_inc(free, 1)
                    if k == 11:
                        taken(act, t, "mean2")
                        act.activation(sq2[:, 0:rw], xc2[:, 0:rw], ACT.Square).then_inc(s_sq2, 1)
                    if k == 14:
                        free = result(act, t, "var2")
                        act.activation(l2[:, 0:rw], bank(t, "var2")[:, 0:rw], ACT.Ln, bias=eps_cols[:, 0:1]
                                       ).then_inc(free, 1)
                        taken(act, t, "var2")
                        act.activation(r2[:, 0:rw], l2[:, 0:rw], ACT.Exp, scale=-0.5).then_inc(s_r2, 1)
                    outs = 0 if rw == 2 else 16 * (BATCH - 2)
                    for use, at, dst, done in (("logit", 17, lg, s_lg_out), ("trh", 23, th, s_th_out),
                                               ("trn", 25, tn, s_tn_out)):
                        if k == at:
                            free = result(act, t, use)
                            if rw == W:
                                need(act, done, t.q * 16 + outs)
                            m, cols_ = (E0, rw) if use == "logit" else (min(rw, TT), NT * D if rw == W else D)
                            act.copy(dst[0:m, 0:cols_], bank(t, use)[0:m, 0:cols_]).then_inc(free, 1)

    def vector(dve):
        dve.memset(mean_w[:], 1.0 / D)
        dve.memset(zero_rows[:], 0.0)
        dve.memset(least[:], -3.0e38)
        dve.memset(eps_cols[:, 0:1], EPS)
        dve.memset(eps_cols[:, 1:2], EPS * EPS / (1 + EPS))
        for s in range(2):
            dve.memset(xr[s][:, :, 0:KC - 1], 0.0)
        dve.memset(carry0[:], 0.0).then_inc(s_const, 1)
        dve.wait_ge(s_const, 1)
        dve.wait_ge(s_weights, 16 * N_WEIGHTS)
        for j in range(2 * NS):
            i = dve.tensor_copy(sel[:, j, :], picks[:, j:j + 1].to_broadcast([P, P]))
        i.then_inc(s_sel, 1)
        dve.wait_ge(s_neg_a, 1)
        dve.tensor_scalar(neg_a[:], neg_a[:], -1.0, None, ALU.mult).then_inc(s_neg_a, 1)
        resets = pairs = 0
        for t in phase_a_turns(dve):
            p, pw, so = t.q + 1, t.pre_w, t.slot ^ 1
            rw, w = t.post_w, t.w
            states = carry0 if t.first else carry[t.slot]

            def keep(k):
                dve.wait_ge(s_scan, t.q * STEPS + (k + 1))
                first = k + 1 - 8
                dve.tensor_copy(states[:, first:k + 1],
                                h[:, first % H_RING:first % H_RING + 8, w - 1:w].rearrange("p k o -> p (k o)")
                                ).then_inc(s_carry, 1)

            for k in range(STEPS + 1):
                if t.scan:
                    if k < STEPS:
                        n, d = divmod(k, 2)
                        if k == 0:
                            dve.wait_ge(s_dtx, t.q + 1)
                        dve.wait_ge(s_b, t.q * NS + (n + 1))
                        need(dve, s_scan, t.q * STEPS + (k - 3))
                        dve.tensor_tensor(dbx[:, k % 4, 0:w], dtx[t.slot][:, d, 0:w], b_bank[n % 2][:, 0:w], ALU.mult
                                          ).then_inc(s_dbx, 1)
                    if k > 0:
                        j = k - 1
                        if j == 0:
                            need(dve, s_carry, t.q * 4 - 4)
                        dve.wait_ge(s_da, t.q * STEPS + (j + 1))
                        dve.wait_ge(s_dbx, t.q * STEPS + (j + 1))
                        need(dve, s_hc, t.q * STEPS + (j + 1 - H_RING))
                        n, d = divmod(j, 2)
                        dve.tensor_tensor_scan(h[:, j % H_RING, 0:w], da[:, j % DA_RING, 0:w], dbx[:, j % 4, 0:w],
                                               0.0 if t.first else states[:, j:j + 1], ALU.mult, ALU.add
                                               ).then_inc(s_scan, 1)
                        if k > 8 and (k - 1) % 8 == 0:
                            keep(k - 2)
                if t.post:
                    if k == 4:
                        dve.wait_ge(s_sum, t.q * STEPS)
                        for d in range(2):
                            dve.tensor_tensor(yz[:, d, 0:rw], sz[so][:, d, 0:rw], y_bank[d][:, 0:rw], ALU.mult
                                              ).then_inc(s_yz, 1)
                    if k == 10:
                        free = result(dve, t, "mean2")
                        dve.tensor_tensor(xc2[:, 0:rw], h1[:, 0:rw], bank(t, "mean2")[:, 0:rw], ALU.subtract
                                          ).then_inc(free, 1)
                    if k == 15:
                        dve.wait_ge(s_r2, t.q)
                        dve.tensor_tensor(n2[:, 0:rw], xc2[:, 0:rw], r2[:, 0:rw], ALU.mult).then_inc(s_n2, 1)
                if t.pre:
                    if k == 4:
                        free = result(dve, t, "mean")
                        need(dve, s_n1, p)
                        dve.tensor_tensor(xc[:, 0:pw], h0[:, 0:pw], bank(t, "mean")[:, 0:pw], ALU.subtract
                                          ).then_inc(free, 1)
                    if k == 8:
                        dve.wait_ge(s_r12, p + 1)
                        dve.scalar_tensor_tensor(out=u[:, 0:pw], in0=xc[:, 0:pw], scalar=(1 + EPS) ** -0.5,
                                                 in1=r12[:, 0:pw], op0=ALU.mult, op1=ALU.mult).then_inc(s_u, 1)
                    if k == 11 and t.fresh:
                        pairs += 1
                        need(dve, s_tail, p)
                        for s in range(2):
                            dve.tensor_copy(xr[s][:, :, 0:KC - 1], tail0[:]).then_inc(s_fresh, 1)
                        dve.wait_ge(s_fresh, 2 * pairs)
                    if k in (12, 13, 14):
                        for d in range(2):
                            if k == 12 and d == 0:
                                need(dve, s_tail, p)
                            if k == 12:
                                dve.wait_ge(s_tap0, p * 2 + (d + 1))
                            else:
                                dve.wait_ge(s_conv_step, p * 4 + (2 * (k - 13) + d + 1))
                            j = 14 - k
                            i = dve.scalar_tensor_tensor(
                                out=cv[:, d, 0:pw], in0=xr[so][:, d, j:j + pw], scalar=taps[:, d * KC + j:d * KC + j + 1],
                                in1=cv[:, d, 0:pw], op0=ALU.mult, op1=ALU.add)
                            i.then_inc(s_conv if k == 14 else s_conv_step, 1)
                    if k == 15:
                        dve.wait_ge(s_conv, (p + 1) * 2)
                        dst = tail0[:] if pw == 2 else xr[so][:, :, 0:KC - 1]
                        dve.tensor_copy(dst, xr[so][:, :, pw:pw + KC - 1]).then_inc(s_tail, 1)
                    if k == 19:
                        dve.wait_ge(s_bch, p + 1)
                        dve.tensor_tensor(bcr[64:128, 0:pw], bank(t, "bc")[64:128, 0:pw], bc[so][64:128, 0:pw],
                                          ALU.subtract).then_inc(s_free[t.bank_of("bc")], 1)
                    if k == 21:
                        dve.wait_ge(s_bcm, p + 1)
                        dve.tensor_tensor(bc[so][96:128, 0:pw], bcr[96:128, 0:pw], bc[so][96:128, 0:pw],
                                          ALU.subtract).then_inc(s_bc, 1)
                    if k == 24:
                        dve.wait_ge(s_spe, p + 1)
                        need(dve, s_spm, p)
                        dve.tensor_scalar(yt[:, :, 0:pw], spe[:, :, 0:pw], 1.0, None, ALU.add).then_inc(s_spu, 1)
                        dve.wait_ge(s_spu, p + 1)
                        dve.scalar_tensor_tensor(out=yt[:, :, 0:pw], in0=yt[:, :, 0:pw], scalar=-1.0,
                                                 in1=spe[:, :, 0:pw], op0=ALU.add, op1=ALU.subtract).then_inc(s_spd, 1)
                    if k == 27:
                        dve.wait_ge(s_spm, p + 1)
                        dve.scalar_tensor_tensor(out=dt[so][:, :, 0:pw], in0=spx[:, :, 0:pw], scalar=0.0,
                                                 in1=spl[:, :, 0:pw], op0=ALU.max, op1=ALU.add).then_inc(s_dt, 1)
            if t.scan:
                keep(STEPS - 1)
            if t.first or t.reset:
                dve.wait_ge(s_carry, 4 * (t.q + 1))
                for s in range(2):
                    dve.tensor_copy(carry[s][:], carry0[:]).then_inc(s_reset, 1)
                resets += 2
                dve.wait_ge(s_reset, resets)

    def gpsimd(pool):
        for t in phase_a_turns(pool):
            p, pw, so = t.q + 1, t.pre_w, t.slot ^ 1
            for k in range(STEPS):
                if t.scan:
                    n, d = divmod(k, 2)
                    pool.wait_ge(s_scan, t.q * STEPS + (k + 1))
                    if d == 0:
                        pool.wait_ge(s_cs, t.q * NS + (n + 1))
                    need(pool, s_sum, t.q * STEPS + (k + 1 - HC_RING))
                    pool.tensor_tensor(hc[:, k % HC_RING, 0:t.w], h[:, k % H_RING, 0:t.w],
                                       cs[:, n % CS_RING, 0:t.w], ALU.mult).then_inc(s_hc, 1)
                if t.pre:
                    if k == 8:
                        pool.wait_ge(s_r1, p + 1)
                        pool.tensor_tensor(n1[:, 0:pw], xc[:, 0:pw], r1[:, 0:pw], ALU.mult).then_inc(s_n1, 1)
                    if k == 9:
                        pool.wait_ge(s_n1, p + 1)
                        pool.tensor_tensor(hn[so][:, 0:pw], h0[:, 0:pw], n1[:, 0:pw], ALU.add).then_inc(s_hn, 1)
                    if k == 25:
                        pool.wait_ge(s_spd, p + 1)
                        pool.wait_ge(s_spl, p + 1)
                        pool.tensor_tensor(spl[:, :, 0:pw], spl[:, :, 0:pw], yt[:, :, 0:pw], ALU.subtract
                                           ).then_inc(s_spm, 1)
                    if k == 28:
                        pool.wait_ge(s_dt, p + 1)
                        pool.tensor_tensor(dtx[so][:, :, 0:pw], dt[so][:, :, 0:pw], xm[:, :, 0:pw], ALU.mult
                                           ).then_inc(s_dtx, 1)

    progs.update(after_a=lambda eng: eng.wait_ge(s_end, 16 * (2 * BATCH + 3)), a_sync=sync, a_scalar=scalar, a_vector=vector, a_gpsimd=gpsimd, a_tensor=tensor)


def phase_b(nc, ctx, mem, a, h_rows, n_rows, logits, after_a, progs):
    def sb(name, shape, dt=F32):
        return mem.enter_context(nc.sbuf_tensor("b_" + name, shape, dt))

    def ps(name, shape, dt=F32):
        return mem.enter_context(nc.psum_tensor("b_" + name, shape, dt))

    def sem(name):
        return ctx.enter_context(nc.semaphore("b_" + name))

    TILES = CAP // P
    FT = FF // P
    ROW_BITS = 14
    MOVE_BITS = 11
    WIDE = CAP + SPAN

    x = sb("x", [P, SPAN])
    tmp = sb("tmp", [P, SPAN])
    tmp_a = sb("tmp_a", [P, SPAN])
    ones = sb("ones", [P, SPAN])
    gt = sb("gt", [P, SPAN])
    eq = sb("eq", [P, SPAN])
    rank = sb("rank", [P, SPAN])
    place = sb("place", [P, SPAN])
    iota = sb("iota", [P, SPAN])
    rows = sb("rows", [P, SPAN], I32)
    chosen = sb("chosen", [P, SPAN], I32)
    entry = sb("entry", [P, SPAN], I32)
    lists = [sb(f"lists{i}", [P, WIDE], I32) for i in range(2)]
    moves = sb("moves", [P, WIDE], I32)
    zeros = sb("zeros", [P, WIDE], I32)
    listf = sb("listf", [P, CAP])
    group = sb("group", [P, P])
    before = sb("before", [P, P])
    first = sb("first", [P, E0])
    member = sb("member", [P, E0])
    ident = sb("ident", [P, P])
    small = sb("small", [P, 16])
    digit, trial, pick = (sb(n, [P, 3], I32) for n in ("digit", "trial", "pick"))
    reach = sb("reach", [P, 3])
    counted = [sb(f"counted{k}", [P, SPAN]) for k in range(3)]
    smalli = sb("smalli", [P, 8], I32)
    row = sb("row", [1, P])
    row8 = sb("row8", [1, E0])
    wide_col = sb("wide_col", [P, 2, P])
    index = sb("index", [P, TILES, E0], U32)
    tab = sb("tab", [P, 3, E0])
    w1 = [sb(f"w1{s}", [P, FF]) for s in range(2)]
    w2 = [sb(f"w2{s}", [P, FT, D]) for s in range(2)]
    b1 = [sb(f"b1{s}", [P, FT]) for s in range(2)]
    b2 = [sb(f"b2{s}", [1, D]) for s in range(2)]
    mine = [sb(f"mine{s}", [P, 3]) for s in range(2)]
    idx = [sb(f"idx{s}", [P, TILES], U32) for s in range(2)]
    xg = [[sb(f"xg{s}_{i}", [P, D]) for i in range(TILES)] for s in range(2)]
    xt = [sb(f"xt{s}", [P, CAP]) for s in range(2)]
    hid = sb("hid", [P, FT, CAP])
    wexp = [sb(f"wexp{s}", [P, TILES]) for s in range(2)]
    og = [[sb(f"og{s}_{i}", [P, D]) for i in range(TILES)] for s in range(2)]

    p_small = ps("p_small", [P, 512])
    p_tr = [ps(f"p_tr{i}", [P, 512]) for i in range(2)]
    p_h = [ps(f"p_h{i}", [P, 512]) for i in range(2)]
    p_o = [ps(f"p_o{i}", [P, 512]) for i in range(2)]
    p_l = ps("p_l", [P, 512])

    s_in, s_dve, s_pe, s_act = sem("in"), sem("dve"), sem("pe"), sem("act")
    s_w = [sem(f"w{s}") for s in range(2)]
    s_lists, s_index = sem("lists"), sem("index")
    s_mine, s_gather, s_tr, s_xt, s_logit, s_wexp, s_hid_mm, s_hid, s_out_mm, s_og, s_scatter = (
        sem("mine"), [sem(f"gather{s}") for s in range(2)], sem("tr"), sem("xt"), sem("logit"), sem("wexp"),
        sem("hid_mm"), sem("hid"), sem("out_mm"), sem("og"), sem("scatter"))
    LOADS = 8
    SEARCH_STEPS, SEARCH_OPS = 16, 9

    def sync(sp):
        after_a(sp)
        for dst, src in ((x[:], logits.rearrange("e (s j) -> (e s) j", s=16)), (rows[:], a["rows"]),
                         (iota[:], a["iota"]), (group[:], a["group"]), (before[:], a["before"]),
                         (first[:], a["first"]), (member[:], a["member"]), (ident[:], a["ident"])):
            sp.dma_start(dst, src).then_inc(s_in, 16)
        sp.dma_start(tab[:, 0, 0:E0], a["w_r"]).then_inc(s_in, 16)
        with sp.Fori(0, E0 // 2) as j:
            for s in range(2):
                e = j * 2 + s
                sp.wait_ge(s_out_mm, e * TILES + TILES)
                sp.dma_start(w1[s][:], a["w1"][ds(e * P, P), :]).then_inc(s_w[s], 16)
                sp.dma_start(w2[s][:].rearrange("p f d -> p (f d)"), a["w2"][ds(e * P, P), :]).then_inc(s_w[s], 16)
                sp.dma_start(b1[s][:], a["b1"][ds(e * P, P), :]).then_inc(s_w[s], 16)
                sp.dma_start(b2[s][:], a["b2"][ds(e, 1), :]).then_inc(s_w[s], 16)

    def vector(dve):
        after_a(dve)
        count = [0]

        def do(i):
            count[0] += 1
            i.then_inc(s_dve, 1)
            dve.wait_ge(s_dve, count[0])

        dve.memset(small[:, 11:12], 0.0).then_inc(s_out_mm, 2 * TILES)
        dve.memset(small[:, 12:13], 0.0).then_inc(s_hid, 2)
        dve.memset(small[:, 13:14], 0.0).then_inc(s_og, 2)
        do(dve.memset(ones[:], 1.0))
        do(dve.memset(zeros[:], 0))
        do(dve.memset(lists[0][:], 0))
        dve.wait_ge(s_in, 16 * (LOADS + 1))
        do(dve.tensor_reduce(small[:, 0:1], x[:], AX.X, ALU.max))
        progs["n_rowmax"] = count[0]
        dve.wait_ge(s_pe, 1)
        do(dve.tensor_reduce(row8[:], p_small[0:1, 0:P].rearrange("o (e s) -> o e s", e=E0), AX.X, ALU.max))
        do(dve.tensor_copy(row[:].rearrange("o (e s) -> o e s", e=E0),
                           row8[:].unsqueeze(2).to_broadcast([1, E0, 16])))
        progs["n_row"] = count[0]
        dve.wait_ge(s_pe, 2)
        do(dve.tensor_scalar(small[:, 1:2], p_small[:, 128:129], -1.0, None, ALU.mult))
        progs["n_negmax"] = count[0]
        do(dve.tensor_scalar(tmp[:], x[:], 0.0, 0.0, ALU.is_ge, ALU.add, accum_out=small[:, 3:4]))
        progs["n_count0"] = count[0]
        dve.wait_ge(s_pe, 3)
        do(dve.tensor_scalar(small[:, 6:7], p_small[:, 129:130], float(CAP), None, ALU.is_ge))
        do(dve.tensor_scalar(smalli[:, 0:1], small[:, 6:7], -1.0, None, ALU.add))
        do(dve.memset(smalli[:, 1:2], 0))
        for k in range(3):
            do(dve.memset(digit[:, k:k + 1], (k + 1) << 29))
        base = count[0]
        progs["n_search"] = base
        STEP = SEARCH_OPS
        with dve.Fori(0, SEARCH_STEPS) as r:
            def step(n, i):
                i.then_inc(s_dve, 1)
                dve.wait_ge(s_dve, r * STEP + (base + n))
            step(1, dve.scalar_tensor_tensor(out=trial[:], in0=digit[:], scalar=smalli[:, 1:2],
                                             in1=smalli[:, 0:1].to_broadcast([P, 3]), op0=ALU.bitwise_or,
                                             op1=ALU.bitwise_xor))
            for k in range(3):
                dve.tensor_scalar(counted[k][:], x[:], trial[:, k:k + 1].bitcast(F32), 0.0, ALU.is_ge, ALU.add,
                                  accum_out=reach[:, k:k + 1]).then_inc(s_dve, 1)
            dve.wait_ge(s_pe, r + 4)
            step(5, dve.tensor_scalar(pick[:], p_small[:, 129:132], float(CAP), -1.0, ALU.is_ge, ALU.mult))
            step(6, dve.tensor_tensor(pick[:], pick[:], digit[:], ALU.bitwise_and))
            step(7, dve.tensor_reduce(smalli[:, 6:7], pick[:], AX.X, ALU.max))
            step(8, dve.tensor_tensor(smalli[:, 1:2], smalli[:, 1:2], smalli[:, 6:7], ALU.bitwise_or))
            step(9, dve.tensor_scalar(digit[:], digit[:], 2, None, ALU.logical_shift_right))
        count[0] = base + SEARCH_STEPS * STEP
        do(dve.tensor_tensor(smalli[:, 4:5], smalli[:, 1:2], smalli[:, 0:1], ALU.bitwise_xor))
        thr = smalli[:, 4:5].bitcast(F32)
        do(dve.tensor_scalar(gt[:], x[:], thr, 0.0, ALU.is_gt, ALU.add, accum_out=small[:, 3:4]))
        do(dve.tensor_scalar(eq[:], x[:], thr, None, ALU.is_equal))
        do(dve.tensor_tensor_scan(rank[:], ones[:], eq[:], 0.0, ALU.mult, ALU.add))
        do(dve.tensor_copy(small[:, 4:5], rank[:, SPAN - 1:SPAN]))
        progs["n_eq"] = count[0]
        dve.wait_ge(s_pe, 5 + SEARCH_STEPS)
        do(dve.tensor_copy(small[:, 8:9], p_small[:, 129:130]))
        do(dve.tensor_tensor(small[:, 9:10], p_small[:, 130:131], small[:, 8:9], ALU.add))
        do(dve.tensor_scalar(rank[:], rank[:], small[:, 9:10], float(CAP), ALU.add, ALU.is_le))
        do(dve.tensor_tensor(eq[:], eq[:], rank[:], ALU.mult))
        do(dve.tensor_tensor(gt[:], gt[:], eq[:], ALU.add))
        do(dve.tensor_copy(chosen[:], gt[:]))
        do(dve.tensor_tensor_scan(rank[:], ones[:], gt[:], 0.0, ALU.mult, ALU.add))
        do(dve.tensor_copy(small[:, 5:6], rank[:, SPAN - 1:SPAN]))
        progs["n_sel"] = count[0]
        dve.wait_ge(s_pe, 7 + SEARCH_STEPS)
        do(dve.tensor_scalar(place[:], rank[:], p_small[:, 131:132], None, ALU.add))
        do(dve.tensor_tensor(place[:], iota[:], place[:], ALU.subtract))
        do(dve.tensor_copy(entry[:], place[:]))
        do(dve.tensor_scalar(entry[:], entry[:], ROW_BITS, None, ALU.logical_shift_left))
        do(dve.tensor_tensor(entry[:], entry[:], rows[:], ALU.bitwise_or))
        do(dve.copy_predicated(lists[0][:, CAP:WIDE], chosen[:], entry[:]))
        for b in range(MOVE_BITS):
            step_ = 1 << b
            lo = max(0, CAP - 2 * step_ + 1)
            cur, new = lists[b % 2], lists[(b + 1) % 2]
            do(dve.tensor_scalar(moves[:, lo:WIDE], cur[:, lo:WIDE], ROW_BITS + b, 1, ALU.logical_shift_right,
                                 ALU.bitwise_and))
            do(dve.tensor_copy(new[:, lo:WIDE], cur[:, lo:WIDE]))
            if b == 0:
                do(dve.memset(lists[1][:, 0:lo], 0))
            do(dve.copy_predicated(new[:, lo:WIDE], moves[:, lo:WIDE], zeros[:, lo:WIDE]))
            do(dve.copy_predicated(new[:, lo:WIDE - step_], moves[:, lo + step_:WIDE], cur[:, lo + step_:WIDE]))
        last = lists[MOVE_BITS % 2]
        do(dve.tensor_scalar(moves[:, 0:CAP], last[:, 0:CAP], (1 << ROW_BITS) - 1, None, ALU.bitwise_and))
        do(dve.tensor_copy(listf[:], moves[:, 0:CAP]))
        progs["n_list"] = count[0]
        do(dve.reciprocal(small[:, 10:11], p_small[:, 132:133]))
        for j, c in enumerate((1, 10)):
            do(dve.tensor_copy(wide_col[:, j, :], small[:, c:c + 1].to_broadcast([P, P])))
        progs["n_wide"] = count[0]
        dve.wait_ge(s_pe, 8 + SEARCH_STEPS)
        do(dve.tensor_copy(tab[:, 1:3, 0:E0], p_small[:, 256:256 + 2 * E0].rearrange("p (j e) -> p j e", j=2)))
        do(dve.tensor_copy(index[:], p_small[:, 192:192 + TILES * E0].rearrange("p (i e) -> p i e", e=E0)))

        def own_columns(e, s):
            need(dve, s_scatter, (e - 1) * 16 * TILES)
            dve.tensor_copy(mine[s][:], tab[:, :, e:e + 1].rearrange("p j o -> p (j o)")).then_inc(s_mine, 1)
            dve.tensor_copy(idx[s][:], index[:, :, e:e + 1].rearrange("p i o -> p (i o)")).then_inc(s_mine, 1)

        own_columns(0, 0)
        for e in range(E0):
            s = e % 2
            for half in range(2):
                dve.wait_ge(s_tr, e * 2 + (half + 1))
                dve.tensor_copy(xt[s][:, half * 512:half * 512 + 512], p_tr[half][:]).then_inc(s_xt, 1)
            if e + 1 < E0:
                own_columns(e + 1, 1 - s)
            dve.wait_ge(s_wexp, e + 1)
            for i in range(TILES):
                dve.wait_ge(s_out_mm, e * TILES + (2 * TILES + i + 1))
                dve.tensor_scalar(og[s][i][:], p_o[i % 2][:, 0:D], wexp[s][:, i:i + 1], mine[s][:, 2:3],
                                  ALU.mult, ALU.mult).then_inc(s_og, 1)

    def scalar(act):
        act.wait_ge(s_dve, progs["n_negmax"])
        act.activation(tmp_a[:], x[:], ACT.Exp, bias=small[:, 1:2], accum_out=small[:, 2:3]).then_inc(s_act, 1)
        act.preload_act_table_set("gelu_and_others")
        with act.Fori(0, E0 // 2) as j:
            for s in range(2):
                e = j * 2 + s
                act.wait_ge(s_w[s], j * 64 + 64)
                for half in range(2):
                    for f in range(FT):
                        g = half * FT + f
                        act.wait_ge(s_hid_mm, e * 2 * FT + (g + 1))
                        act.activation(hid[:, f, half * 512:half * 512 + 512], p_h[f % 2][:], ACT.Gelu,
                                       bias=b1[s][:, f:f + 1]).then_inc(s_hid, 1)
                act.wait_ge(s_mine, e * 2 + 2)
                act.wait_ge(s_logit, e + 1)
                act.activation(wexp[s][:], p_l[:, 0:TILES], ACT.Exp, bias=mine[s][:, 1:2]).then_inc(s_wexp, 1)
                act.preload_act_table_set("gelu_and_others")

    def tensor(pe):
        pe.wait_ge(s_dve, progs["n_rowmax"])
        pe.matmul(p_small[0:1, 0:P], small[:, 0:1], ident[:], start=True, stop=True).then_inc(s_pe, 1)
        pe.wait_ge(s_dve, progs["n_row"])
        pe.matmul(p_small[:, 128:129], row[:], ones[0:1, 0:1], start=True, stop=True).then_inc(s_pe, 1)
        pe.wait_ge(s_dve, progs["n_count0"])
        pe.matmul(p_small[:, 129:130], group[:], small[:, 3:4], start=True, stop=True).then_inc(s_pe, 1)
        with pe.Fori(0, SEARCH_STEPS) as r:
            pe.wait_ge(s_dve, r * SEARCH_OPS + (progs["n_search"] + 4))
            pe.matmul(p_small[:, 129:132], group[:], reach[:], start=True, stop=True).then_inc(s_pe, 1)
        pe.wait_ge(s_dve, progs["n_eq"])
        pe.matmul(p_small[:, 129:130], group[:], small[:, 3:4], start=True, stop=True).then_inc(s_pe, 1)
        pe.matmul(p_small[:, 130:131], before[:], small[:, 4:5], start=True, stop=True).then_inc(s_pe, 1)
        pe.wait_ge(s_dve, progs["n_sel"])
        pe.matmul(p_small[:, 131:132], before[:], small[:, 5:6], start=True, stop=True).then_inc(s_pe, 1)
        pe.wait_ge(s_act, 1)
        pe.matmul(p_small[:, 132:133], group[:], small[:, 2:3], start=True, stop=True).then_inc(s_pe, 1)
        pe.wait_ge(s_dve, progs["n_wide"])
        for i in range(TILES):
            pe.matmul(p_small[:, 192 + i * E0:192 + (i + 1) * E0], listf[:, i * P:(i + 1) * P], member[:],
                      start=True, stop=True)
        for j in range(2):
            mm = pe.matmul(p_small[:, 256 + j * E0:256 + (j + 1) * E0], wide_col[:, j, :], first[:],
                           start=True, stop=True)
        mm.then_inc(s_pe, 1)
        with pe.Fori(0, E0 // 2) as j:
            for s in range(2):
                e = j * 2 + s
                pe.wait_ge(s_gather[s], j * (16 * TILES) + 16 * TILES)
                for half in range(2):
                    for i in range(4):
                        mm = pe.transpose(p_tr[half][:, i * P:(i + 1) * P], xg[s][half * 4 + i][:], ident[:])
                    mm.then_inc(s_tr, 1)
                pe.wait_ge(s_xt, e * 2 + 2)
                pe.wait_ge(s_mine, e * 2 + 2)
                for i in range(TILES):
                    mm = pe.matmul(p_l[:, i:i + 1], xt[s][:, i * P:(i + 1) * P], mine[s][:, 0:1], start=True, stop=True)
                mm.then_inc(s_logit, 1)
                pe.wait_ge(s_w[s], j * 64 + 64)
                for half in range(2):
                    for f in range(FT):
                        g = half * FT + f
                        pe.wait_ge(s_hid, e * 2 * FT + (g + 1))
                        pe.matmul(p_h[f % 2][:], w1[s][:, f * P:(f + 1) * P], xt[s][:, half * 512:half * 512 + 512],
                                  start=True, stop=True).then_inc(s_hid_mm, 1)
                pe.wait_ge(s_hid, e * 2 * FT + (2 * FT + 2))
                for i in range(TILES):
                    pe.wait_ge(s_og, e * TILES + (i + 1))
                    pe.matmul(p_o[i % 2][:, 0:D], ones[0:1, 0:P], b2[s][:], start=True, stop=False)
                    for f in range(FT):
                        mm = pe.matmul(p_o[i % 2][:, 0:D], hid[:, f, i * P:(i + 1) * P], w2[s][:, f, :],
                                       start=False, stop=(f == FT - 1))
                    mm.then_inc(s_out_mm, 1)

    def gpsimd(pool):
        def gather(e, s):
            pool.wait_ge(s_mine, e * 2 + 2)
            for i in range(TILES):
                pool.indirect_dma_start(xg[s][i][:], None, n_rows[:, :],
                                        bass.IndirectOffsetOnAxis(ap=idx[s][:, i:i + 1], axis=0)
                                        ).then_inc(s_gather[s], 16)
        def scatter(e, s):
            need(pool, s_scatter, e * 16 * TILES)
            for i in range(TILES):
                pool.wait_ge(s_og, e * TILES + (i + 3))
                pool.indirect_dma_start(h_rows[:, :], bass.IndirectOffsetOnAxis(ap=idx[s][:, i:i + 1], axis=0),
                                        og[s][i][:], None, compute_op=ALU.add).then_inc(s_scatter, 16)

        gather(0, 0)
        for e in range(E0):
            if e + 1 < E0:
                gather(e + 1, (e + 1) % 2)
            scatter(e, e % 2)

    progs.update(b_sync=sync, b_scalar=scalar, b_vector=vector, b_gpsimd=gpsimd, b_tensor=tensor)
    return lambda eng: eng.wait_ge(s_scatter, 16 * TILES * E0)


GT = 4
GW = GT * P
NG = BATCH * RPI // GW
NH, DH = 8, 16
WIN = 64
E1, EG = 8, 4
HF = 256
NGATE = 2 + E1


class Group:

    def __init__(self, i, slot, n):
        self.i, self.slot, self.n = i, slot, n
        self.n_before = n if slot else n - 1


def phase_c_turns(engine):
    def at(c, j=None):
        if j is None:
            return Group(c, c % 2, c // 2 + 1) if 0 <= c < NG else None
        return Group(j * 2 + c, c % 2, j + (c // 2 + 1))

    for b in range(-3, 2):
        yield [at(b + k) for k in range(4)]
    with engine.Fori(0, (NG - 5) // 2) as j:
        for b in range(2, 4):
            yield [at(b + k, j) for k in range(4)]
    for b in range(NG - 3, NG):
        yield [at(b + k) for k in range(4)]


def phase_c(nc, ctx, mem, a, h_rows, out, after_b, progs):
    def sb(name, shape, dt=F32):
        return mem.enter_context(nc.sbuf_tensor("c_" + name, shape, dt))

    def ps(name, shape, dt=F32):
        return mem.enter_context(nc.psum_tensor("c_" + name, shape, dt))

    def sem(name):
        return ctx.enter_context(nc.semaphore("c_" + name))

    ident, mean_w = sb("ident", [P, P]), sb("mean_w", [P, P])
    w_qkv = sb("w_qkv", [P, 3 * D])
    w_proj = sb("w_proj", [P, D])
    w_up = sb("w_up", [P, 4 * HF])
    w_so = sb("w_so", [P, 2, D])
    w_ex = sb("w_ex", [P, 2, E1 * D])
    w_gate = sb("w_gate", [P, NGATE])
    gate_b = sb("gate_b", [1, NGATE])
    bias9 = sb("bias9", [E1 + 1, D])
    cols = sb("cols", [P, 3])
    eps_cols = sb("eps_cols", [P, 2])
    ones = sb("ones", [1, P])
    earlier = sb("earlier", [P, GT, EG, EG])
    later = sb("later", [P, GT, EG, EG])

    x = [sb(f"x{s}", [P, GT, D]) for s in range(2)]
    stats, mv = sb("stats", [P, GT, 6]), sb("mv", [P, GT, 2])
    marker = sb("marker", [1, 1])
    lnv, rstd = sb("lnv", [P, GT]), sb("rstd", [P, GT])
    n3 = sb("n3", [P, GT, D])
    nt = sb("nt", [P, GW])
    qkv = sb("qkv", [P, GT, 3 * D])
    prod = [sb(f"prod{j}", [P, NH * NH * DH]) for j in range(GT)]
    score = sb("score", [P, GT * NH, NH])
    top = sb("top", [P, GT * NH])
    expo = sb("expo", [P, GT * NH, NH])
    denom = sb("denom", [P, GT * NH])
    prob = sb("prob", [P, GT * NH, NH])
    o = sb("o", [P, GT, D])
    ot = sb("ot", [P, 8, GT * 16])
    dealt = [sb(f"dealt{s}", [P, NH, GT * 16]) for s in range(2)]
    xc, sq, lv, r12, u = (sb(n, [P, GW]) for n in ("xc", "sq", "lv", "r12", "u"))
    h3, fl = ([sb(f"{n}{s}", [P, GW]) for s in range(2)] for n in ("h3", "fl"))
    act_half = [sb(f"act_half{i}", [P, GW]) for i in range(2)]
    hid = [sb(f"hid{i}", [P, GW]) for i in range(4)]
    gate = sb("gate", [P, GT, NGATE])
    in1, in0 = sb("in1", [P, GT, 1]), sb("in0", [P, GT, 1])
    ea, eb, esel, eexp, ep, etop = (sb(n, [P, GT, EG]) for n in ("ea", "eb", "esel", "eexp", "ep", "etop"))
    gmax, gsum, ginv, tsum, tinv = (sb(n, [P, GT]) for n in ("gmax", "gsum", "ginv", "tsum", "tinv"))
    ge, gtt, rk = (sb(n, [P, GT, EG, EG]) for n in ("ge", "gtt", "rk"))
    rank, sel, share = (sb(n, [P, GT, EG]) for n in ("rank", "sel", "share"))
    comb = sb("comb", [P, GT, E1])
    cnt = sb("cnt", [P, GT, E1 + 1])
    cntt = sb("cntt", [E1 + 1, GW])
    base = sb("base", [P, GT, D])
    acc = [sb(f"acc{i}", [P, D]) for i in range(2)]
    res = [sb(f"res{s}", [P, GT, D]) for s in range(2)]

    heads = [nc.dram_tensor(f"heads{s}", [P, 8, GT * 16], F32, kind="Internal").ap() for s in range(2)]

    p_turn, p_gate, p_qkv, p_m = (ps(n, [P, 512]) for n in ("p_turn", "p_gate", "p_qkv", "p_m"))
    p_w = [ps(f"p_w{i}", [P, 512]) for i in range(2)]
    p_e = [ps(f"p_e{i}", [P, 512]) for i in range(2)]

    s_in, s_const = sem("in"), sem("const")
    s_x, s_heads, s_dealt, s_res = ([sem(f"{n}{s}") for s in range(2)] for n in ("x", "heads", "dealt", "res"))
    s_stats, s_mv, s_lnv, s_rstd, s_n3, s_n3t, s_nt, s_qkv_mm, s_qkv = map(
        sem, ("stats", "mv", "lnv", "rstd", "n3", "n3t", "nt", "qkv_mm", "qkv"))
    s_qk, s_score, s_top, s_dif, s_exp, s_den, s_inv, s_prob, s_pv, s_o, s_o_t, s_ot = map(
        sem, ("qk", "score", "top", "dif", "exp", "den", "inv", "prob", "pv", "o", "o_t", "ot"))
    s_proj, s_h3, s_mean, s_xc, s_sq, s_var, s_lv, s_r12, s_u, s_fl = map(
        sem, ("proj", "h3", "mean", "xc", "sq", "var", "lv", "r12", "u", "fl"))
    s_up, s_silu, s_hid, s_gate_mm, s_route, s_gexp, s_cnt_t, s_cntt, s_base_mm, s_base, s_ex, s_acc = map(
        sem, ("up", "silu", "hid", "gate_mm", "route", "gexp", "cnt_t", "cntt", "base_mm", "base", "ex", "acc"))
    LOADS = 13
    R_DIF, R_CNT, R_END = 8, 24, 24

    def sync(sp):
        after_b(sp)
        for dst, name in ((ident, "ident"), (w_qkv, "w_qkv"), (w_proj, "w_proj"), (w_up, "w_up"), (w_gate, "w_gate"),
                          (gate_b, "gate_b"), (bias9, "bias9"), (cols, "cols_c"), (w_so, "w_so"), (w_ex, "w_ex"),
                          (earlier, "earlier"), (later, "later")):
            sp.dma_start(dst[:], a[name]).then_inc(s_in, 16)
        sp.dma_start(ones[:], a["ones"]).then_inc(s_in, 16)
        for E, N, A, L in phase_c_turns(sp):
            if N:
                sp.wait_ge(s_ot, N.i + 1)
                sp.dma_start(heads[N.slot], ot[:]).then_inc(s_heads[N.slot], 16)
                sp.wait_ge(s_heads[N.slot], N.n * 16)
                for j in range(8):
                    sp.dma_start(dealt[N.slot][j * DH:(j + 1) * DH, :, :],
                                 heads[N.slot][:, j, :].rearrange("(h d) c -> d h c", d=DH)
                                 ).then_inc(s_dealt[N.slot], 16)
            if L:
                need(sp, s_proj, L.i - 1)
                sp.dma_start(x[L.slot][:], h_rows[ds(L.i * GW + SHIFT, GW), :].rearrange("(j p) d -> p j d", p=P)
                             ).then_inc(s_x[L.slot], 16)
            if E:
                sp.wait_ge(s_acc, E.i * (9 * GT) + 9 * GT)
                sp.dma_start(out[ds(E.i * GW, GW), :].rearrange("(j p) d -> p j d", p=P), res[E.slot][:]
                             ).then_inc(s_res[E.slot], 16)
        for s in range(2):
            sp.wait_ge(s_res[s], 16 * ((NG + 1 - s) // 2))

    def tensor(pe):
        pe.wait_ge(s_in, 16 * LOADS)
        pe.wait_ge(s_const, 1)
        for E, N, A, L in phase_c_turns(pe):
            def turn_n3():
                if A:
                    pe.wait_ge(s_n3, A.i + 1)
                    need(pe, s_ot, A.i - 1)
                    for j in range(GT):
                        mm = pe.transpose(p_turn[:, j * P:(j + 1) * P], n3[:, j, :], ident[:])
                    mm.then_inc(s_n3t, 1)

            def qkv_mm(j):
                if A:
                    pe.wait_ge(s_nt, A.i + 1)
                    need(pe, s_qkv, A.i * GT + j)
                    pe.matmul(p_qkv[:, 0:3 * D], nt[:, j * P:(j + 1) * P], w_qkv[:], start=True, stop=True
                              ).then_inc(s_qkv_mm, 1)

            def turn_o():
                if N:
                    pe.wait_ge(s_o, N.i * GT + GT)
                    if A:
                        pe.wait_ge(s_nt, A.i + 1)
                    for j in range(GT):
                        mm = pe.transpose(p_turn[:, j * P:(j + 1) * P], o[:, j, :], ident[:])
                    mm.then_inc(s_o_t, 1)

            def project():
                if N:
                    pe.wait_ge(s_dealt[N.slot], N.n * (16 * 8))
                    need(pe, s_lv, N.i)
                    pe.matmul(p_m[:].rearrange("c (w h a) -> c w h a", h=NH, a=8), w_proj[:],
                              dealt[N.slot][:].rearrange("p h (w a) -> p w h a", a=8), start=True, stop=False,
                              skip_group_check=True)
                    for j in range(GT):
                        mm = pe.matmul(p_m[:, j * P:(j + 1) * P], x[N.slot][:, j, :], ident[:], start=False,
                                       stop=(j == GT - 1), skip_group_check=True)
                    mm.then_inc(s_proj, 1)

            def mean():
                if N:
                    pe.wait_ge(s_h3, N.i + 1)
                    pe.matmul(p_m[:], mean_w[:], h3[N.slot][:], start=True, stop=True).then_inc(s_mean, 1)

            def variance():
                if N:
                    pe.wait_ge(s_sq, N.i + 1)
                    pe.matmul(p_m[:], mean_w[:], sq[:], start=True, stop=True).then_inc(s_var, 1)

            def up(i):
                for m in (2 * i, 2 * i + 1) if E else ():
                    if m == 0:
                        pe.wait_ge(s_fl, E.i + 1)
                    if m < 2:
                        need(pe, s_base, E.i * GT)
                    need(pe, s_hid if m % 2 else s_silu, E.i * 4 + i)
                    pe.matmul(p_w[m % 2][:], w_up[:, m * P:(m + 1) * P], fl[E.slot][:], start=True, stop=True
                              ).then_inc(s_up, 1)

            def gates():
                if E:
                    need(pe, s_cntt, E.i)
                    for j in range(GT):
                        pe.matmul(p_gate[:, j * 16:j * 16 + NGATE], fl[E.slot][:, j * P:(j + 1) * P], w_gate[:],
                                  start=True, stop=False)
                        mm = pe.matmul(p_gate[:, j * 16:j * 16 + NGATE], ones[:], gate_b[:], start=False, stop=True)
                    mm.then_inc(s_gate_mm, 1)

            def experts(j, half):
                if E:
                    if j == 0:
                        pe.wait_ge(s_hid, E.i * 4 + 4)
                    need(pe, s_acc, E.i * (9 * GT) + 9 * (j - 1) + 4 * (half + 1))
                    for k in range(2):
                        mm = pe.matmul(p_e[half][:], hid[2 + k][:, j * P:(j + 1) * P],
                                       w_ex[:, k, half * 512:half * 512 + 512], start=(k == 0), stop=(k == 1))
                    mm.then_inc(s_ex, 1)

            def turn_counts():
                if E:
                    pe.wait_ge(s_route, E.i * R_END + R_CNT)
                    for j in range(GT):
                        mm = pe.transpose(p_gate[0:E1 + 1, j * P:(j + 1) * P], cnt[:, j, :], ident[:])
                    mm.then_inc(s_cnt_t, 1)

            def base_mm(j):
                if E:
                    if j == 0:
                        pe.wait_ge(s_cntt, E.i + 1)
                    if j >= 2:
                        pe.wait_ge(s_base, E.i * GT + (j - 1))
                    w = p_w[j % 2][:, 0:D]
                    pe.matmul(w, cntt[:, j * P:(j + 1) * P], bias9[:], start=True, stop=False)
                    for k in range(2):
                        pe.matmul(w, hid[k][:, j * P:(j + 1) * P], w_so[:, k, :], start=False, stop=False)
                    pe.matmul(w, h3[E.slot][:, j * P:(j + 1) * P], ident[:], start=False, stop=True
                              ).then_inc(s_base_mm, 1)

            up(0)
            turn_n3()
            gates()
            up(1)
            qkv_mm(0)
            turn_o()
            up(2)
            qkv_mm(1)
            up(3)
            experts(0, 0)
            qkv_mm(2)
            experts(0, 1)
            qkv_mm(3)
            turn_counts()
            base_mm(0)
            base_mm(1)
            project()
            experts(1, 0)
            mean()
            experts(1, 1)
            base_mm(2)
            base_mm(3)
            experts(2, 0)
            variance()
            experts(2, 1)
            experts(3, 0)
            experts(3, 1)

    def scalar(act):
        act.wait_ge(s_in, 16 * LOADS)
        act.wait_ge(s_const, 1)
        act.preload_act_table_set("natural_log_exp_and_others")
        for E, N, A, L in phase_c_turns(act):
            def silu(i):
                if E:
                    act.wait_ge(s_up, E.i * 8 + (2 * i + 1))
                    need(act, s_hid, E.i * 4 + (i - 1))
                    act.activation(act_half[i % 2][:], p_w[0][:], ACT.Silu).then_inc(s_silu, 1)

            def qkv_copy(j):
                if A:
                    act.wait_ge(s_qkv_mm, A.i * GT + (j + 1))
                    need(act, s_pv, A.i * GT)
                    act.copy(qkv[:, j, :], p_qkv[:, 0:3 * D]).then_inc(s_qkv, 1)

            def base_copy(j):
                if E:
                    act.wait_ge(s_base_mm, E.i * GT + (j + 1))
                    act.copy(base[:, j, :], p_w[j % 2][:, 0:D]).then_inc(s_base, 1)

            silu(0)
            if A:
                act.wait_ge(s_n3t, A.i + 1)
                act.copy(nt[:], p_turn[:]).then_inc(s_nt, 1)
            silu(1)
            qkv_copy(0)
            if N:
                act.wait_ge(s_o_t, N.i + 1)
                need(act, s_heads[1 - N.slot], N.n_before * 16)
                act.copy(ot[:].rearrange("p j c -> p c j"), p_turn[:].rearrange("p (c j) -> p c j", j=8)
                         ).then_inc(s_ot, 1)
            silu(2)
            qkv_copy(1)
            silu(3)
            if E:
                act.preload_act_table_set("natural_log_exp_and_others")
                act.wait_ge(s_route, E.i * R_END + R_DIF)
                act.activation(eexp[:], esel[:], ACT.Exp).then_inc(s_gexp, 1)
            qkv_copy(2)
            qkv_copy(3)
            if E:
                act.wait_ge(s_cnt_t, E.i + 1)
                act.copy(cntt[:], p_gate[0:E1 + 1, :]).then_inc(s_cntt, 1)
            base_copy(0)
            base_copy(1)
            if N:
                act.wait_ge(s_proj, N.i + 1)
                need(act, s_base_mm, N.i * GT - GT)
                act.activation(h3[N.slot][:], p_m[:], ACT.Identity, bias=cols[:, 0:1]).then_inc(s_h3, 1)
            if A:
                act.wait_ge(s_dif, A.i + 1)
                act.activation(expo[:], score[:], ACT.Exp, scale=DH ** -0.5).then_inc(s_exp, 1)
            if N:
                act.wait_ge(s_xc, N.i + 1)
                act.activation(sq[:], xc[:], ACT.Square).then_inc(s_sq, 1)
            base_copy(2)
            base_copy(3)
            if N:
                act.wait_ge(s_var, N.i + 1)
                act.activation(lv[:], p_m[:], ACT.Ln, bias=eps_cols[:, 1:2]).then_inc(s_lv, 1)
                act.wait_ge(s_lv, N.i + 1)
                act.activation(r12[:], lv[:], ACT.Exp, scale=-0.5).then_inc(s_r12, 1)
                act.wait_ge(s_u, N.i + 1)
                act.activation(fl[N.slot][:], u[:], ACT.Identity, scale=cols[:, 1:2], bias=cols[:, 2:3]
                               ).then_inc(s_fl, 1)
            if L:
                act.wait_ge(s_mv, L.i + 1)
                act.activation(lnv[:], mv[:, :, 1], ACT.Ln, bias=eps_cols[:, 0:1]).then_inc(s_lnv, 1)
                act.wait_ge(s_lnv, L.i + 1)
                act.activation(rstd[:], lnv[:], ACT.Exp, scale=-0.5).then_inc(s_rstd, 1)
            if N:
                act.preload_act_table_set("silu_and_others")

    def vector(dve):
        dve.memset(mean_w[:], 1.0 / D)
        dve.memset(eps_cols[:, 0:1], EPS)
        dve.memset(cnt[:, :, E1:E1 + 1], 1.0)
        dve.memset(eps_cols[:, 1:2], EPS * EPS / (1 + EPS)).then_inc(s_const, 1)
        dve.wait_ge(s_in, 16 * LOADS)
        wide = [P, GT, EG]
        square = [P, GT, EG, EG]
        heads2 = [P, GT * NH, NH]
        for E, N, A, L in phase_c_turns(dve):
            steps = [0]

            def do(i):
                steps[0] += 1
                i.then_inc(s_route, 1)
                dve.wait_ge(s_route, E.i * R_END + steps[0])

            def norm():
                dve.wait_ge(s_x[L.slot], L.n * 16)
                for j in range(GT):
                    i = dve.bn_stats(stats[:, j, :], x[L.slot][:, j, :])
                i.then_inc(s_stats, 1)
                dve.wait_ge(s_stats, L.i + 1)
                dve.memset(marker[:], 0.0)
                for j in range(GT):
                    i = dve.bn_aggr(mv[:, j, :], stats[:, j, :])
                i.then_inc(s_mv, 1)
                dve.wait_ge(s_rstd, L.i + 1)
                dve.wait_ge(s_mv, L.i + 1)
                need(dve, s_n3t, L.i)
                for j in range(GT):
                    i = dve.tensor_scalar(n3[:, j, :], x[L.slot][:, j, :], mv[:, j, 0:1], rstd[:, j:j + 1],
                                          ALU.subtract, ALU.mult)
                i.then_inc(s_n3, 1)

            def hidden(i):
                if E:
                    dve.wait_ge(s_silu, E.i * 4 + (i + 1))
                    dve.wait_ge(s_up, E.i * 8 + (2 * i + 2))
                    dve.tensor_tensor(hid[i][:], act_half[i % 2][:], p_w[1][:], ALU.mult).then_inc(s_hid, 1)

            def sum_scores(j):
                if A:
                    dve.wait_ge(s_qk, A.i * GT + (j + 1))
                    dve.tensor_reduce(score[:, j * NH:(j + 1) * NH, :],
                                      prod[j][:].rearrange("p (h g d) -> p h g d", h=NH, g=NH), AX.X, ALU.add
                                      ).then_inc(s_score, 1)

            def less_top():
                if A:
                    dve.wait_ge(s_score, A.i * GT + GT)
                    dve.tensor_reduce(top[:], score[:], AX.X, ALU.max).then_inc(s_top, 1)
                    dve.wait_ge(s_top, A.i + 1)
                    dve.tensor_tensor(score[:], score[:], top[:].unsqueeze(2).to_broadcast(heads2), ALU.subtract
                                      ).then_inc(s_dif, 1)

            def probs():
                if A:
                    dve.wait_ge(s_exp, A.i + 1)
                    dve.tensor_reduce(denom[:], expo[:], AX.X, ALU.add).then_inc(s_den, 1)
                    dve.wait_ge(s_den, A.i + 1)
                    dve.reciprocal(denom[:], denom[:]).then_inc(s_inv, 1)
                    dve.wait_ge(s_inv, A.i + 1)
                    dve.tensor_tensor(prob[:], expo[:], denom[:].unsqueeze(2).to_broadcast(heads2), ALU.mult
                                      ).then_inc(s_prob, 1)

            def sum_values(G, j):
                if G:
                    dve.wait_ge(s_pv, G.i * GT + (j + 1))
                    need(dve, s_o_t, G.i)
                    dve.tensor_reduce(o[:, j, :], prod[j][:].rearrange("p (h g) -> p h g", g=NH), AX.X, ALU.add
                                      ).then_inc(s_o, 1)

            def choose_group():
                dve.wait_ge(s_gate_mm, E.i + 1)
                do(dve.tensor_copy(gate[:], p_gate[:, 0:GT * 16].rearrange("p (j k) -> p j k", k=16)[:, :, 0:NGATE]))
                do(dve.tensor_tensor(in1[:], gate[:, :, 1:2], gate[:, :, 0:1], ALU.is_gt))
                do(dve.tensor_scalar(in0[:], in1[:], -1.0, 1.0, ALU.mult, ALU.add))
                do(dve.tensor_tensor(ea[:], gate[:, :, 2:2 + EG], in0[:].to_broadcast(wide), ALU.mult))
                do(dve.tensor_tensor(eb[:], gate[:, :, 2 + EG:2 + 2 * EG], in1[:].to_broadcast(wide), ALU.mult))
                do(dve.tensor_tensor(ea[:], ea[:], eb[:], ALU.add))
                do(dve.tensor_reduce(gmax[:], ea[:], AX.X, ALU.max))
                do(dve.tensor_tensor(esel[:], ea[:], gmax[:].unsqueeze(2).to_broadcast(wide), ALU.subtract))
                assert steps[0] == R_DIF

            def choose_experts():
                dve.wait_ge(s_gexp, E.i + 1)
                do(dve.tensor_reduce(gsum[:], eexp[:], AX.X, ALU.add))
                do(dve.reciprocal(ginv[:], gsum[:]))
                do(dve.tensor_tensor(ep[:], eexp[:], ginv[:].unsqueeze(2).to_broadcast(wide), ALU.mult))
                other = ep[:].unsqueeze(2).to_broadcast(square)
                own = ep[:].unsqueeze(3).to_broadcast(square)
                do(dve.tensor_tensor(ge[:], other, own, ALU.is_ge))
                do(dve.tensor_tensor(gtt[:], other, own, ALU.is_gt))
                do(dve.tensor_tensor(ge[:], ge[:], earlier[:], ALU.mult))
                do(dve.tensor_tensor(gtt[:], gtt[:], later[:], ALU.mult))
                do(dve.tensor_tensor(rk[:], ge[:], gtt[:], ALU.add))
                do(dve.tensor_reduce(rank[:], rk[:], AX.X, ALU.add))
                do(dve.tensor_scalar(sel[:], rank[:], 2.0, None, ALU.is_lt))
                do(dve.tensor_tensor(etop[:], ep[:], sel[:], ALU.mult))
                do(dve.tensor_reduce(tsum[:], etop[:], AX.X, ALU.add))
                do(dve.tensor_scalar(tsum[:], tsum[:], 1e-8, None, ALU.add))
                do(dve.reciprocal(tinv[:], tsum[:]))
                do(dve.tensor_tensor(share[:], etop[:], tinv[:].unsqueeze(2).to_broadcast(wide), ALU.mult))
                dve.tensor_tensor(cnt[:, :, 0:EG], sel[:], in0[:].to_broadcast(wide), ALU.mult)
                dve.tensor_tensor(cnt[:, :, EG:E1], sel[:], in1[:].to_broadcast(wide), ALU.mult)
                dve.tensor_tensor(comb[:, :, 0:EG], share[:], in0[:].to_broadcast(wide), ALU.mult)
                do(dve.tensor_tensor(comb[:, :, EG:E1], share[:], in1[:].to_broadcast(wide), ALU.mult))
                assert steps[0] == R_END

            def add_experts(j, half):
                if not E:
                    return
                c0 = E.i * (9 * GT) + 9 * j
                dve.wait_ge(s_ex, E.i * (2 * GT) + (2 * j + half + 1))
                for e in range(half * EG, half * EG + EG):
                    y = p_e[half][:, e % EG * D:(e % EG + 1) * D]
                    w = comb[:, j, e:e + 1]
                    if e == 1:
                        dve.tensor_scalar(acc[1][:], y, w, None, ALU.mult).then_inc(s_acc, 1)
                        continue
                    if e == 0:
                        dve.wait_ge(s_base, E.i * GT + (j + 1))
                    else:
                        dve.wait_ge(s_acc, c0 + (e - 1))
                    dve.scalar_tensor_tensor(out=acc[e % 2][:], in0=y, scalar=w,
                                             in1=base[:, j, :] if e == 0 else acc[e % 2][:], op0=ALU.mult,
                                             op1=ALU.add).then_inc(s_acc, 1)
                if half:
                    if j == 0:
                        need(dve, s_res[E.slot], E.n * 16 - 16)
                    dve.wait_ge(s_acc, c0 + 8)
                    dve.tensor_tensor(res[E.slot][:, j, :], acc[0][:], acc[1][:], ALU.add).then_inc(s_acc, 1)
                    dve.wait_ge(s_acc, c0 + 9)

            hidden(0)
            sum_values(N, 2)
            hidden(1)
            sum_values(N, 3)
            if E:
                choose_group()
            hidden(2)
            hidden(3)
            if E:
                choose_experts()
            sum_scores(0)
            sum_scores(1)
            sum_scores(2)
            add_experts(0, 0)
            add_experts(0, 1)
            sum_scores(3)
            less_top()
            add_experts(1, 0)
            probs()
            if N:
                dve.wait_ge(s_mean, N.i + 1)
                dve.tensor_tensor(xc[:], h3[N.slot][:], p_m[:], ALU.subtract).then_inc(s_xc, 1)
            add_experts(1, 1)
            add_experts(2, 0)
            add_experts(2, 1)
            if N:
                dve.wait_ge(s_r12, N.i + 1)
                dve.wait_ge(s_xc, N.i + 1)
                dve.scalar_tensor_tensor(out=u[:], in0=xc[:], scalar=(1 + EPS) ** -0.5, in1=r12[:], op0=ALU.mult,
                                         op1=ALU.mult).then_inc(s_u, 1)
            if L:
                norm()
            add_experts(3, 0)
            sum_values(A, 0)
            add_experts(3, 1)
            sum_values(A, 1)

    def gpsimd(pool):
        for E, N, A, L in phase_c_turns(pool):
            for j in range(GT) if A else ():
                pool.wait_ge(s_qkv, A.i * GT + (j + 1))
                need(pool, s_o, A.i * GT + (j + 1 - GT))
                q, k = qkv[:, j, 0:D], qkv[:, j, D:2 * D]
                pool.tensor_tensor(prod[j][:].rearrange("p (h g d) -> p h g d", h=NH, g=NH),
                                   q.rearrange("p (h d) -> p h d", d=DH).unsqueeze(2).to_broadcast([P, NH, NH, DH]),
                                   k.rearrange("p (g d) -> p g d", d=DH).unsqueeze(1).to_broadcast([P, NH, NH, DH]),
                                   ALU.mult).then_inc(s_qk, 1)
            for j in range(GT) if A else ():
                pool.wait_ge(s_prob, A.i + 1)
                v = qkv[:, j, 2 * D:3 * D]
                pool.tensor_tensor(prod[j][:].rearrange("p (h d g) -> p h d g", h=NH, g=NH),
                                   prob[:, j * NH:(j + 1) * NH, :].unsqueeze(2).to_broadcast([P, NH, DH, NH]),
                                   v.rearrange("p (g d) -> p d g", d=DH).unsqueeze(1).to_broadcast([P, NH, DH, NH]),
                                   ALU.mult).then_inc(s_pv, 1)

    progs.update(c_sync=sync, c_scalar=scalar, c_vector=vector, c_gpsimd=gpsimd, c_tensor=tensor)


def lay_out(i):
    f = {k: np.asarray(v) for k, v in i.items()}
    x = f["x"].reshape(BATCH, 3, 56, 4, 56, 4).transpose(1, 3, 5, 0, 2, 4).reshape(PV, BATCH * NPATCH)
    halves = lambda v: v.reshape(2, P, -1).transpose(1, 0, 2)
    wbc = np.concatenate([f["L0_attn_W_B"], f["L0_attn_W_C"]], 0)
    z = np.zeros_like(wbc)
    wbc = halves(np.concatenate([wbc, z, wbc, wbc], 0).T)
    cols = np.concatenate([
        f["L0_tok_b"][:, None], f["cls_tok"].reshape(D, 1), f["L0_tok_cls"].reshape(D, 1),
        f["L0_attn_ln_g"][:, None], f["L0_attn_ln_b"][:, None], f["L0_attn_conv_b"].reshape(2, P).T,
        f["L0_attn_b_dt"].reshape(2, P).T, halves(f["L0_attn_conv_w"].reshape(DI, KC)).reshape(P, 2 * KC),
        halves(f["L0_attn_log_A"]).reshape(P, 2 * NS)], 1)
    picks = np.zeros((P, 2 * NS), np.float32)
    for first in (0, 64, 96):
        picks[first:first + 2 * NS] = np.eye(2 * NS)
    m = {"patches": x, "wtok": f["L0_tok_W"].T, "cols": cols, "w_in": f["L0_attn_W_in"].T,
         "ident": np.eye(P, dtype=np.float32), "picks": picks, "w_bc": wbc, "w_dt": halves(f["L0_attn_W_dt"].T),
         "w_out": halves(f["L0_attn_W_out"].T), "w_r": f["L0_ffn_Wr"]}
    part, col = np.arange(P)[:, None], np.arange(SPAN)[None, :]
    token = np.minimum(part % 16 * SPAN + col, NTOK - 1)
    image, t = token // T, token % T
    m["rows"] = (image * RB + np.where(t < SHIFT, t + T, t)).astype(np.int32)
    m["iota"] = np.broadcast_to(CAP + 1 + col, (P, SPAN)).astype(np.float32)
    q = np.arange(P)
    same = q[:, None] // 16 == q[None, :] // 16
    m["group"] = same.astype(np.float32)
    m["before"] = (same & (q[:, None] < q[None, :])).astype(np.float32)
    m["member"] = (q[:, None] // 16 == np.arange(E0)[None, :]).astype(np.float32)
    m["first"] = (q[:, None] == 16 * np.arange(E0)[None, :]).astype(np.float32)
    m["w1"] = f["L0_ffn_W1"].reshape(E0 * D, FF)
    m["w2"] = f["L0_ffn_W2"].reshape(E0, FF // P, P, D).transpose(0, 2, 1, 3).reshape(E0 * P, FF)
    m["b1"] = f["L0_ffn_b1"].reshape(E0, FF // P, P).transpose(0, 2, 1).reshape(E0 * P, FF // P)
    m["b2"] = f["L0_ffn_b2"]
    m["w_qkv"] = f["L1_attn_w_qkv"].T
    m["w_proj"] = f["L1_attn_w_proj"].T
    pairs = lambda v: v.reshape(2, 2, P, D).transpose(1, 0, 2, 3).reshape(4 * P, D)
    m["w_up"] = np.concatenate([pairs(f["L1_ffn_shared_in_w"]), pairs(f["L1_ffn_expert_in_w"])], 0).T
    m["w_so"] = halves(f["L1_ffn_shared_out_w"].T)
    m["w_ex"] = halves(f["L1_ffn_expert_out_weight"].transpose(2, 0, 1).reshape(HF, E1 * D))
    m["w_gate"] = np.concatenate([f["L1_ffn_group_gate_w"], f["L1_ffn_expert_gate_w"]], 0).T
    m["gate_b"] = np.concatenate([f["L1_ffn_group_bias"], f["L1_ffn_expert_bias"]])[None]
    m["bias9"] = np.concatenate([f["L1_ffn_expert_out_bias"], f["L1_ffn_shared_out_b"][None]], 0)
    m["cols_c"] = np.stack([f["L1_attn_b_proj"], f["L1_ffn_ln_scale"], f["L1_ffn_ln_bias"]], 1)
    e = np.arange(EG)
    m["earlier"] = np.broadcast_to(e[None, :] < e[:, None], (P, GT, EG, EG)).astype(np.float32)
    m["later"] = np.broadcast_to(e[None, :] > e[:, None], (P, GT, EG, EG)).astype(np.float32)
    m["ones"] = np.ones((1, P), np.float32)
    return {k: np.ascontiguousarray(v) for k, v in m.items()}


def kernel(**inputs):
    import concourse.bacc as bacc
    from concourse.bass_utils import run_bass_kernel_spmd

    nc = bacc.Bacc("TRN2", target_bir_lowering=False, num_devices=1)
    arrays = lay_out(inputs)
    args = {k: nc.dram_tensor(f"in_{k}", v.shape, mybir.dt.from_np(v.dtype), kind="ExternalInput").ap()
            for k, v in arrays.items()}
    rolled = nc.dram_tensor("rolled", (BATCH * RPI, D), F32, kind="ExternalOutput").ap()
    build(nc, args, rolled)
    r = run_bass_kernel_spmd(nc, [{f"in_{k}": v for k, v in arrays.items()}], core_ids=[0])
    got = r.results[0]["rolled"].reshape(BATCH, RPI, D)[:, :T]
    return np.concatenate([got[:, T - SHIFT:], got[:, :T - SHIFT]], 1)
```
